# Optimizing a Trainium2 kernel written in Bass

```python
import numpy as np
import jax
import jax.numpy as jnp

def _softmax(x, axis=-1):
    return jax.nn.softmax(x, axis=axis)

def _gelu(x):
    return jax.nn.gelu(x, approximate=True)

def _silu(x):
    return jax.nn.silu(x)

def _sigmoid(x):
    return jax.nn.sigmoid(x)

def _layernorm(x, axis=-1, eps=1e-05):
    m = jnp.mean(x, axis=axis, keepdims=True)
    v = jnp.var(x, axis=axis, keepdims=True)
    return (x - m) / jnp.sqrt(v + eps)

def _scatter_add(tgt, idx, src, axis=0):
    return tgt.at[idx].add(src)

def _segment_sum(src, seg, n):
    return jax.ops.segment_sum(src, seg, n)
kernel_name = 'mk_audio_tower_d1_tok_audfeat256_r4_b0be01'

def setup_inputs(seed: int=0):
    np.random.seed(seed)
    _w = jnp.asarray

    def _rec_inputs():
        import jax
        import jax.numpy as jnp
        _rk = jax.random.key(seed)
        x = 7.22013e-05 + 1.00017 * jax.random.normal(jax.random.fold_in(_rk, 1), (8, 750, 64), jnp.float32)
        return x
    x = _rec_inputs()

    def _L0_tok_setup():
        import jax, jax.numpy as jnp
        import numpy as np
        B, T, D = (8, 1024, 64)
        N_RECUR = 2
        TW = 15
        STRIDE = 2
        key = jax.random.key(seed)
        ks = jax.random.split(key, 8)
        glorot = (2.0 / (D + D)) ** 0.5
        X = jax.random.normal(ks[0], (B, T, D), dtype=jnp.float32)
        W_in = jax.random.normal(ks[1], (N_RECUR, D, D), dtype=jnp.float32) * glorot
        b_in = jax.random.normal(ks[2], (N_RECUR, D), dtype=jnp.float32) * 0.05
        W_out = jax.random.normal(ks[3], (N_RECUR, D, D), dtype=jnp.float32) * glorot
        b_out = jax.random.normal(ks[4], (N_RECUR, D), dtype=jnp.float32) * 0.05
        core_diag = jnp.ones((D,), dtype=jnp.float32)
        conv_filter = jax.random.normal(ks[5], (TW,), dtype=jnp.float32) * (2.0 / (TW + 1)) ** 0.5
        return {'X': X, 'W_in': W_in, 'b_in': b_in, 'W_out': W_out, 'b_out': b_out, 'core_diag': core_diag, 'conv_filter': conv_filter, 'stride': STRIDE}
    _L0_tok_all = _L0_tok_setup()
    _L0_tok_in = {k: v for k, v in _L0_tok_all.items() if k in ('W_in', 'b_in', 'W_out', 'b_out', 'core_diag', 'conv_filter')}
    del _L0_tok_all

    def _L0_attn_setup():
        import jax, jax.numpy as jnp
        import numpy as np
        B, L, D = (4, 1024, 64)
        key = jax.random.key(seed)
        kx, kq, kk, kv, ko = jax.random.split(key, 5)
        std = 0.02
        return {'x': jax.random.normal(kx, (B, L, D), dtype=jnp.float32), 'Wq': std * jax.random.normal(kq, (D, D), dtype=jnp.float32), 'Wk': std * jax.random.normal(kk, (D, D), dtype=jnp.float32), 'Wv': std * jax.random.normal(kv, (D, D), dtype=jnp.float32), 'Wo': std * jax.random.normal(ko, (D, D), dtype=jnp.float32)}
    _L0_attn_all = _L0_attn_setup()
    _L0_attn_in = {k: v for k, v in _L0_attn_all.items() if k in ('Wq', 'Wk', 'Wv', 'Wo')}
    del _L0_attn_all

    def _L0_ffn_setup():
        import jax, jax.numpy as jnp
        import numpy as np
        B, S, H, F, E, K = (8, 1024, 64, 128, 16, 2)
        EPS = 1e-05
        key = jax.random.key(seed)
        ks = jax.random.split(key, 9)
        sc = 0.02
        return {'x': jax.random.normal(ks[0], (B, S, H), dtype=jnp.float32), 'gate_w': jax.random.normal(ks[1], (H, E), dtype=jnp.float32) * sc, 'gate_b': jnp.zeros((E,), dtype=jnp.float32), 'w1': jax.random.normal(ks[2], (E, H, F), dtype=jnp.float32) * sc, 'b1': jnp.zeros((E, F), dtype=jnp.float32), 'w2': jax.random.normal(ks[3], (E, F, H), dtype=jnp.float32) * sc, 'b2': jnp.zeros((E, H), dtype=jnp.float32), 'gamma': jnp.ones((H,), dtype=jnp.float32), 'beta': jnp.zeros((H,), dtype=jnp.float32)}
    _L0_ffn_all = _L0_ffn_setup()
    _L0_ffn_in = {k: v for k, v in _L0_ffn_all.items() if k in ('gate_w', 'gate_b', 'w1', 'b1', 'w2', 'b2', 'gamma', 'beta')}
    del _L0_ffn_all
    return {'x': x, 'L0_tok_W_in': _L0_tok_in['W_in'], 'L0_tok_b_in': _L0_tok_in['b_in'], 'L0_tok_W_out': _L0_tok_in['W_out'], 'L0_tok_b_out': _L0_tok_in['b_out'], 'L0_tok_core_diag': _L0_tok_in['core_diag'], 'L0_tok_conv_filter': _L0_tok_in['conv_filter'], 'L0_attn_Wq': _L0_attn_in['Wq'], 'L0_attn_Wk': _L0_attn_in['Wk'], 'L0_attn_Wv': _L0_attn_in['Wv'], 'L0_attn_Wo': _L0_attn_in['Wo'], 'L0_ffn_gate_w': _L0_ffn_in['gate_w'], 'L0_ffn_gate_b': _L0_ffn_in['gate_b'], 'L0_ffn_w1': _L0_ffn_in['w1'], 'L0_ffn_b1': _L0_ffn_in['b1'], 'L0_ffn_w2': _L0_ffn_in['w2'], 'L0_ffn_b2': _L0_ffn_in['b2'], 'L0_ffn_gamma': _L0_ffn_in['gamma'], 'L0_ffn_beta': _L0_ffn_in['beta']}

def reference(x, L0_tok_W_in, L0_tok_b_in, L0_tok_W_out, L0_tok_b_out, L0_tok_core_diag, L0_tok_conv_filter, L0_attn_Wq, L0_attn_Wk, L0_attn_Wv, L0_attn_Wo, L0_ffn_gate_w, L0_ffn_gate_b, L0_ffn_w1, L0_ffn_b1, L0_ffn_w2, L0_ffn_b2, L0_ffn_gamma, L0_ffn_beta):
    import jax
    import jax.numpy as jnp

    def _L0_tok_ref(X, W_in, b_in, W_out, b_out, core_diag, conv_filter, stride):
        import jax, jax.numpy as jnp
        import numpy as np
        B, T, D = (8, 1024, 64)
        N_RECUR = 2
        TW = 15
        STRIDE = 2
        out = X
        for i in range(W_in.shape[0]):
            out = jnp.tanh(out @ W_in[i] + b_in[i])
        out = jnp.abs(core_diag)[None, None, :] * out * out
        n = W_out.shape[0]
        for i in range(n):
            out = jnp.tanh(out @ W_out[n - 1 - i] + b_out[n - 1 - i])
        tw = conv_filter.shape[0]
        pad = tw // 2
        out = jnp.pad(out, ((0, 0), (pad, pad), (0, 0)))
        d = out.shape[-1]
        kernel = jnp.broadcast_to(conv_filter[:, None, None], (tw, 1, d))
        out_pool = jax.lax.conv_general_dilated(out, kernel, window_strides=(stride,), padding='VALID', dimension_numbers=('NWC', 'WIO', 'NWC'), feature_group_count=d)
        return out_pool

    def _L0_attn_ref(x, Wq, Wk, Wv, Wo):
        import jax, jax.numpy as jnp
        import numpy as np
        B, L, D = (4, 1024, 64)
        q = x @ Wq.T
        k = x @ Wk.T
        v = x @ Wv.T
        logits = jnp.einsum('bld,bmd->blm', q, k)
        Lq = x.shape[1]
        causal_mask = jnp.triu(jnp.ones((Lq, Lq), dtype=bool), k=1)
        logits = jnp.where(causal_mask[None], jnp.asarray(0.0, logits.dtype), logits)
        attn = jax.nn.relu(logits)
        row_counts = jnp.maximum(jnp.arange(Lq, dtype=attn.dtype), 1.0)
        attn = attn / row_counts[None, :, None]
        ctx = jnp.einsum('blm,bmd->bld', attn, v)
        return ctx @ Wo.T

    def _L0_ffn_ref(x, gate_w, gate_b, w1, b1, w2, b2, gamma, beta):
        import jax, jax.numpy as jnp
        import numpy as np
        B, S, H, F, E, K = (8, 1024, 64, 128, 16, 2)
        EPS = 1e-05
        gate_logits = x @ gate_w + gate_b
        topk_vals, topk_idx = jax.lax.top_k(gate_logits, K)
        topk_w = jax.nn.softmax(topk_vals, axis=-1)
        h = jax.nn.relu(jnp.einsum('bsh,ehf->bsef', x, w1) + b1)
        expert_out = jnp.einsum('bsef,efh->bseh', h, w2) + b2
        sel = jnp.take_along_axis(expert_out, topk_idx[:, :, :, None], axis=2)
        moe = jnp.sum(topk_w[..., None] * sel, axis=2)
        y = x + moe
        mu = jnp.mean(y, axis=-1, keepdims=True)
        var = jnp.var(y, axis=-1, keepdims=True)
        return (y - mu) / jnp.sqrt(var + EPS) * gamma + beta
    h = _L0_tok_ref(x, L0_tok_W_in, L0_tok_b_in, L0_tok_W_out, L0_tok_b_out, L0_tok_core_diag, L0_tok_conv_filter, 2)
    h = h + _L0_attn_ref(_layernorm(h, axis=-1), L0_attn_Wq, L0_attn_Wk, L0_attn_Wv, L0_attn_Wo)
    h = h + _L0_ffn_ref(_layernorm(h, axis=-1), L0_ffn_gate_w, L0_ffn_gate_b, L0_ffn_w1, L0_ffn_b1, L0_ffn_w2, L0_ffn_b2, L0_ffn_gamma, L0_ffn_beta)
    return h

_drawn_inputs = setup_inputs


def setup_inputs(seed=0):
    import zlib

    import numpy as np

    out = dict(_drawn_inputs(seed))
    spreads = {'L0_tok_core_diag': (1.0, 0.2),
     'L0_ffn_gate_b': (0.0, 0.1),
     'L0_ffn_b1': (0.0, 0.8),
     'L0_ffn_b2': (0.0, 0.494),
     'L0_ffn_gamma': (1.0, 0.2),
     'L0_ffn_beta': (0.0, 0.299)}
    factors = {'L0_attn_Wq': 6.118,
     'L0_attn_Wk': 8.0,
     'L0_attn_Wv': 8.0,
     'L0_attn_Wo': 8.0,
     'L0_ffn_w1': 5.176,
     'L0_ffn_w2': 4.126}
    for name, (base, spread) in spreads.items():
        noise = np.random.default_rng([zlib.crc32(name.encode()), seed]).standard_normal(out[name].shape)
        drawn = base * np.exp(spread * noise) if base else spread * noise
        out[name] = jnp.asarray(drawn.astype(out[name].dtype))
    for name, factor in factors.items():
        out[name] = (out[name] * factor).astype(out[name].dtype)
    return out
```

```python
from contextlib import ExitStack

import concourse.bass as bass
from concourse import mybir

F32 = mybir.dt.float32
F32R = mybir.dt.float32r
I32 = mybir.dt.int32
ALU = mybir.AluOpType
ACT = mybir.ActivationFunctionType
AX = mybir.AxisListType

P = 128
TOK = 125
PAIR = 2
BIG = 3.0e38
EPS = 1e-5


class Signal:

    def __init__(self, sem, per, unit=1):
        self.sem, self.per, self.unit = sem, per, unit

    def after(self, g, k):
        return (self.per * g + k) * self.unit


def audio_tower(nc, x, w_in, b_in, w_out, b_out, core, filt, wq, wk, wv, wo,
                gate_w, gate_b, w1, b1, w2, b2, gamma, beta, out):
    B, T, D = x.shape
    TO = out.shape[1]
    E, _, F = w1.shape
    NG = B // PAIR
    NT = T // TOK
    NR = TO // TOK
    NJ = NR * PAIR
    HT = T // 2
    W = TO + 1
    TAPS = filt.shape[0]
    assert D * PAIR == P and F == P and T == 2 * TO and HT == NR * TOK

    ctx = ExitStack()
    with ctx:
        def sb(name, shape, dt=F32):
            return ctx.enter_context(nc.sbuf_tensor(name, shape, dt))

        def bank(name):
            return ctx.enter_context(nc.psum_tensor(name, [P, 512], F32))

        def sem(name):
            return ctx.enter_context(nc.semaphore(name))

        def signal(name, per=1, unit=1):
            return Signal(sem(name), per, unit)

        ident = sb("ident", [P, P])
        w_tok = sb("w_tok", [P, 4, P])
        bias_tok = sb("bias_tok", [P, 3])
        bias_last = sb("bias_last", [TOK, PAIR, D])
        core_col = sb("core_col", [P, 1])
        core_abs = sb("core_abs", [P, 1])
        filt_row = sb("filt_row", [1, 768])
        filt_pad = nc.dram_tensor("filt_pad", [1, 768], F32)
        band = sb("band", [TOK, 640])
        conv_w = sb("conv_w", [TOK, 4, TOK])
        wq2 = sb("wq2", [D, PAIR, D])
        wk_s = sb("wk_s", [D, D])
        wv2 = sb("wv2", [D, PAIR, D])
        wo_s = sb("wo_s", [D, D])
        wo_t = sb("wo_t", [D, D])
        w_qk = sb("w_qk", [P, P])
        w_vo = sb("w_vo", [P, P])
        minus_half = sb("minus_half", [TOK, NJ])
        causal_cap = sb("causal_cap", [TOK, TOK])
        row_pos = sb("row_pos", [TOK, NR], I32)
        row_cnt = sb("row_cnt", [TOK, NR])
        row_inv = sb("row_inv", [TOK, NR])
        prio_i = sb("prio_i", [TOK, E], I32)
        prio = sb("prio", [TOK, 1, E])
        gate_w2 = sb("gate_w2", [P, E])
        gate_bb = sb("gate_bb", [TOK, 1, E])
        w1_raw = sb("w1_raw", [P, E, F])
        w1_hi = sb("w1_hi", [P, E, F], F32R)
        w1_lo = sb("w1_lo", [P, E, F], F32R)
        w2_s = sb("w2_s", [F, E, D])
        b1_s = sb("b1_s", [E, F])
        b1_col = sb("b1_col", [F, E])
        b2_diag = sb("b2_diag", [NJ * E, NJ, D])
        gamma_b = sb("gamma_b", [TOK, 1, D])
        beta_b = sb("beta_b", [TOK, 1, D])

        x_in = sb("x_in", [TOK, NT, PAIR, D])
        x_t = sb("x_t", [P, T])
        act1 = sb("act1", [P, T])
        act2 = sb("act2", [P, T])
        sq = sb("sq", [P, T])
        act3 = sb("act3", [P, T])
        pre4 = sb("pre4", [TOK, NT, P])
        act4 = sb("act4", [TOK, NT, P])
        hres = sb("hres", [TOK, NJ, D])
        xc = sb("xc", [TOK, NJ, D])
        xsq = sb("xsq", [TOK, NJ, D])
        stat = sb("stat", [TOK, 4, NJ])
        xn1 = sb("xn1", [TOK, NJ, D])
        xn1_t = sb("xn1_t", [P, TO])
        q_t = sb("q_t", [P, TO])
        v_s = sb("v_s", [TOK, NR, P])
        attn = sb("attn", [TOK, PAIR, NJ * TOK])
        h2 = sb("h2", [TOK, NJ, D])
        xn2 = sb("xn2", [TOK, NJ, D])
        split = sb("split", [TOK, NJ, 2, D], F32R)
        xg = sb("xg", [P, PAIR, W], F32R)
        logits = sb("logits", [TOK, NJ, E])
        top = sb("top", [TOK, 8, NJ])
        pick1 = sb("pick1", [TOK, NJ, E])
        pick2 = sb("pick2", [TOK, NJ, E])
        work = sb("work", [TOK, 4, NJ, E])
        gates_new = sb("gates_new", [TOK, NJ, E])
        gates_t = sb("gates_t", [NJ * E, TOK])
        y_base = sb("y_base", [TOK, NJ, D])
        xs = sb("xs", [P, PAIR, W], F32R)
        gates = sb("gates", [TOK, NJ, E])
        h2_m = sb("h2_m", [TOK, NJ, D])
        hid = sb("hid", [F, 2, PAIR, W])
        prod = sb("prod", [TOK, 2, NJ, D])
        acc = sb("acc", [TOK, NJ, D])
        yc = sb("yc", [TOK, NJ, D])
        ysq = sb("ysq", [TOK, NJ, D])
        ystat = sb("ystat", [TOK, 4, NJ])
        yn = sb("yn", [TOK, NJ, D])
        y_out = sb("y_out", [TOK, NJ, D])

        z = [bank("z0"), bank("z1")]
        y = [bank("y0"), bank("y1")]
        pa, pb, pc, pd = bank("pa"), bank("pb"), bank("pc"), bank("pd")

        ld_tok = sem("ld_tok")
        ld_filt = sem("ld_filt")
        ld_band = sem("ld_band")
        ld_attn = sem("ld_attn")
        ld_gate = sem("ld_gate")
        ld_w1 = sem("ld_w1")
        ld_w2 = sem("ld_w2")
        zeroed = sem("zeroed")
        const_pool = sem("const_pool")
        pool_chain = sem("pool_chain")
        const_dve = sem("const_dve")
        set_pe = sem("set_pe")
        w1_ready = sem("w1_ready")
        x_in_ready = signal("x_in_ready", PAIR, 16)
        x_turned = signal("x_turned", 2)
        xt_act = signal("xt_act")
        xt_dve = signal("xt_dve")
        mm1 = signal("mm1", 2)
        tanh1 = signal("tanh1", 2)
        mm2 = signal("mm2", 2)
        tanh2 = signal("tanh2", 2)
        squared_d = signal("squared_d")
        squared_p = signal("squared_p")
        mm3 = signal("mm3", 2)
        tanh3 = signal("tanh3", 2)
        mm4 = signal("mm4", 2)
        biased4 = signal("biased4", 2)
        tanh4 = signal("tanh4")
        conv_done = signal("conv_done")
        ln1_done = signal("ln1_done")
        var_ready = signal("var_ready", 2)
        rstd_ready = signal("rstd_ready", 2)
        yvar_ready = signal("yvar_ready")
        yrstd_ready = signal("yrstd_ready")
        xn1_turned = signal("xn1_turned")
        xn1t_ready = signal("xn1t_ready")
        qv_done = signal("qv_done", 2)
        qt_ready = signal("qt_ready")
        v_ready = signal("v_ready")
        logit_done = signal("logit_done", PAIR)
        off_ready = signal("off_ready", 2 * PAIR)
        diag_ready = signal("diag_ready", NR * PAIR)
        ctx_done = signal("ctx_done")
        ln2_done = signal("ln2_done")
        split_turned = signal("split_turned", PAIR)
        xg_act = signal("xg_act")
        xg_dve = signal("xg_dve")
        gate_done = signal("gate_done")
        diff_ready = signal("diff_ready")
        exp_ready = signal("exp_ready")
        gates_made = signal("gates_made")
        gates_turned = signal("gates_turned")
        gates_t_ready = signal("gates_t_ready")
        b2_done = signal("b2_done")
        y_base_ready = signal("y_base_ready")
        handed = signal("handed", 3)
        z_done = signal("z_done", PAIR * E)
        relu_done = signal("relu_done", PAIR * E)
        y_done = signal("y_done", E)
        gated = signal("gated", E)
        summed = signal("summed", E)
        acc_read = signal("acc_read")
        y_out_ready = signal("y_out_ready")
        stored = signal("stored", PAIR, 16)
        ta_chain = signal("ta_chain", 31)
        fin_chain = signal("fin_chain", 7)

        block = ctx.enter_context(nc.Block())
        halves = [slice(0, HT), slice(HT, T)]
        MID = 368
        BANDW = MID + TAPS // 2 + 2 * TOK + 1
        ROW = 768
        assert BANDW + TOK <= ROW and MID + TAPS // 2 >= 3 * TOK

        def conv_block(k):
            top_col = MID + TAPS // 2 + TOK * (k - 1)
            return band[:, top_col:top_col - 2 * TOK:-2]

        @block.sync
        def _(sp):
            def load_x(g):
                for b in range(PAIR):
                    src = x[PAIR * g + b].rearrange("(c p) d -> p c d", p=TOK)
                    sp.dma_start(x_in[:, :, b, :], src).then_inc(x_in_ready.sem, 16)

            def store(g):
                sp.wait_ge(y_out_ready.sem, y_out_ready.after(g, 1))
                view = y_out[:].rearrange("p (r b) d -> p r b d", b=PAIR)
                for b in range(PAIR):
                    dst = out[PAIR * g + b].rearrange("(r p) d -> p r d", p=TOK)
                    sp.dma_start(dst, view[:, :, b, :]).then_inc(stored.sem, 16)

            load_x(0)
            sp.wait_ge(zeroed, 1)
            layers = [w_in[0], w_in[1], w_out[1], w_out[0]]
            for n, w in enumerate(layers):
                for b in range(PAIR):
                    sp.dma_start(w_tok[b * D:(b + 1) * D, n, b * D:(b + 1) * D], w).then_inc(ld_tok, 16)
            sp.wait_ge(zeroed, 3)
            for j in range(NJ):
                sp.dma_start(b2_diag[j * E:(j + 1) * E, j, :], b2).then_inc(ld_gate, 16)
            for b in range(PAIR):
                sp.dma_start(gate_w2[b * D:(b + 1) * D, :], gate_w).then_inc(ld_gate, 16)
            sp.dma_start(gate_bb[:, 0, :], gate_b.partition_broadcast(TOK)).then_inc(ld_gate, 16)
            sp.dma_start(gamma_b[:, 0, :], gamma.partition_broadcast(TOK)).then_inc(ld_gate, 16)
            sp.dma_start(beta_b[:, 0, :], beta.partition_broadcast(TOK)).then_inc(ld_gate, 16)
            for g in range(1, NG):
                sp.wait_ge(x_turned.sem, x_turned.after(g - 1, 2))
                load_x(g)
                if g >= 2:
                    store(g - 2)
            store(NG - 2)
            store(NG - 1)
            sp.wait_ge(stored.sem, stored.after(NG - 1, PAIR))

        @block.scalar
        def _(act):
            for n, bv in enumerate([b_in[0], b_in[1], b_out[1]]):
                for b in range(PAIR):
                    act.dma_start(bias_tok[b * D:(b + 1) * D, n:n + 1], bv.unsqueeze(1)).then_inc(ld_tok, 16)
            for b in range(PAIR):
                act.dma_start(bias_last[:, b, :], b_out[0].partition_broadcast(TOK)).then_inc(ld_tok, 16)
                act.dma_start(core_col[b * D:(b + 1) * D, :], core.unsqueeze(1)).then_inc(ld_tok, 16)
                act.dma_start(wq2[:, b, :], wq).then_inc(ld_attn, 16)
                act.dma_start(wv2[:, b, :], wv).then_inc(ld_attn, 16)
            act.dma_start(wk_s[:], wk).then_inc(ld_attn, 16)
            act.dma_start(wo_s[:], wo).then_inc(ld_attn, 16)
            act.dma_start(b1_s[:], b1).then_inc(ld_attn, 16)
            for b in range(PAIR):
                act.dma_start(w1_raw[b * D:(b + 1) * D, :, :], w1.rearrange("e h f -> h e f")).then_inc(ld_w1, 16)
            act.dma_start(w2_s[:], w2.rearrange("e f h -> f e h")).then_inc(ld_w2, 16)

            def step(s, g):
                if s == 0:
                    act.wait_ge(x_turned.sem, x_turned.after(g, 1))
                    act.copy(x_t[:, halves[0]], pa[:, 0:HT]).then_inc(xt_act.sem, 1)
                elif s in (1, 2, 3):
                    done, src, dst, said = {1: (mm1, (pc, pd), act1, tanh1), 2: (mm2, (pa, pb), act2, tanh2),
                                            3: (mm3, (pc, pd), act3, tanh3)}[s]
                    for h in range(2):
                        act.wait_ge(done.sem, done.after(g, h + 1))
                        act.activation(dst[:, halves[h]], src[h][:, 0:HT], ACT.Tanh,
                                       bias=bias_tok[:, s - 1:s]).then_inc(said.sem, 1)
                elif s == 4:
                    act.wait_ge(biased4.sem, biased4.after(g, 2))
                    act.activation(act4[:], pre4[:], ACT.Tanh).then_inc(tanh4.sem, 1)
                elif s == 7:
                    act.wait_ge(xn1_turned.sem, xn1_turned.after(g, 1))
                    act.copy(xn1_t[:], pd[:, 0:TO]).then_inc(xn1t_ready.sem, 1)
                elif s == 8:
                    act.wait_ge(qv_done.sem, qv_done.after(g, 1))
                    act.copy(q_t[:], pa[:, 0:TO]).then_inc(qt_ready.sem, 1)
                elif s == 9:
                    for b, (p0, p1) in enumerate([(pa, pb), (pc, pd)]):
                        act.wait_ge(logit_done.sem, logit_done.after(g, b + 1))
                        act.activation(attn[:, b, TOK:TO], p0[0:TOK, TOK:TO], ACT.Relu).then_inc(off_ready.sem, 1)
                        act.wait_ge(diag_ready.sem, diag_ready.after(g, NR * b + 1))
                        act.activation(attn[:, b, TO + TOK:TO + 2 * TOK], p1[0:TOK, TOK:2 * TOK],
                                       ACT.Relu).then_inc(off_ready.sem, 1)
                elif s == 12:
                    act.wait_ge(split_turned.sem, split_turned.after(g, 1))
                    act.copy(xg[:, 0, 0:TO], pb[:, 0:TO]).then_inc(xg_act.sem, 1)
                elif s == 14:
                    act.wait_ge(diff_ready.sem, diff_ready.after(g, 1))
                    act.activation(top[:, 3, :], top[:, 2, :], ACT.Exp).then_inc(exp_ready.sem, 1)
                elif s == 15:
                    act.wait_ge(gates_turned.sem, gates_turned.after(g, 1))
                    act.copy(gates_t[:], pa[0:NJ * E, 0:TOK]).then_inc(gates_t_ready.sem, 1)

            def experts(g, e):
                for b in range(PAIR):
                    act.wait_ge(z_done.sem, z_done.after(g, PAIR * e + b + 1))
                    if g or e >= 2:
                        act.wait_ge(y_done.sem, y_done.after(g, max(e - 1, 0)))
                    act.activation(hid[:, e % 2, b, 0:TO], z[b][:, 0:TO], ACT.Relu,
                                   bias=b1_col[:, e:e + 1]).then_inc(relu_done.sem, 1)

            act.wait_ge(ld_w1, 32)
            act.copy(w1_hi[:], w1_raw[:]).then_inc(w1_ready, 1)
            act.wait_ge(ld_tok, 16 * 18)
            for s in range(17):
                step(s, 0)
            act.wait_ge(const_dve, 5)
            for g in range(NG):
                for e in range(E):
                    experts(g, e)
                    if g + 1 < NG:
                        step(e, g + 1)

        @block.gpsimd
        def _(pool):
            made = [0]

            def chain(ins):
                made[0] += 1
                ins.then_inc(pool_chain, 1)
                pool.wait_ge(pool_chain, made[0])

            nc.gpsimd.memset(w_tok[:], 0.0).then_inc(zeroed, 1)
            nc.gpsimd.memset(filt_row[:], 0.0).then_inc(zeroed, 1)
            nc.gpsimd.memset(b2_diag[:], 0.0).then_inc(zeroed, 1)
            nc.gpsimd.memset(w_qk[:], 0.0).then_inc(zeroed, 1)
            nc.gpsimd.memset(w_vo[:], 0.0).then_inc(zeroed, 1)
            pool.wait_ge(zeroed, 2)
            pool.dma_start(filt_row[0:1, MID:MID + TAPS], filt.unsqueeze(0)).then_inc(ld_filt, 16)
            chain(nc.gpsimd.memset(ident[:], 0.0))
            nc.gpsimd.affine_select(out=ident[:], in_=ident[:], compare_op=ALU.not_equal, fill=1.0, base=0,
                                    pattern=[[-1, P]], channel_multiplier=1).then_inc(const_pool, 1)
            pool.wait_ge(ld_filt, 16)
            pool.dma_start(filt_pad[:], filt_row[:]).then_inc(ld_filt, 16)
            pool.wait_ge(ld_filt, 32)
            shifts = bass.AP(filt_pad, 0, [[1, TOK], [1, BANDW]])
            pool.dma_start(band[:, 0:BANDW], shifts).then_inc(ld_band, 16)
            chain(nc.gpsimd.memset(causal_cap[:], BIG))
            nc.gpsimd.affine_select(out=causal_cap[:], in_=causal_cap[:], compare_op=ALU.is_ge, fill=0.0, base=0,
                                    pattern=[[1, TOK]], channel_multiplier=-1).then_inc(const_pool, 1)
            nc.gpsimd.iota(row_pos[:], pattern=[[TOK, NR]], base=0, channel_multiplier=1).then_inc(const_pool, 1)
            nc.gpsimd.iota(prio_i[:], pattern=[[-1, E]], base=E, channel_multiplier=0).then_inc(const_pool, 1)
            nc.gpsimd.memset(minus_half[:], -0.5).then_inc(const_pool, 1)
            nc.gpsimd.memset(xg[:, :, TO:W].bitcast(F32), 0.0).then_inc(const_pool, 1)

            def step(s, g):
                if s == 2:
                    pool.wait_ge(tanh2.sem, tanh2.after(g, 2))
                    if g:
                        pool.wait_ge(mm3.sem, mm3.after(g - 1, 2))
                    nc.gpsimd.tensor_tensor(sq[:, halves[1]], act2[:, halves[1]], act2[:, halves[1]],
                                            ALU.mult).then_inc(squared_p.sem, 1)
                elif s in (5, 10):
                    n = 1 if s == 5 else 2
                    pool.wait_ge(var_ready.sem, var_ready.after(g, n))
                    nc.gpsimd.tensor_tensor(stat[:, 3, :], stat[:, 2, :], minus_half[:],
                                            ALU.pow).then_inc(rstd_ready.sem, 1)

            def finish(g):
                pool.wait_ge(yvar_ready.sem, yvar_ready.after(g, 1))
                nc.gpsimd.tensor_tensor(ystat[:, 3, :], ystat[:, 2, :], minus_half[:],
                                        ALU.pow).then_inc(yrstd_ready.sem, 1)

            def experts(g, e):
                pool.wait_ge(gated.sem, gated.after(g, e + 1))
                if e == 0:
                    pool.wait_ge(y_base_ready.sem, y_base_ready.after(g, 1))
                    if g:
                        pool.wait_ge(acc_read.sem, acc_read.after(g - 1, 1))
                    prev = y_base
                else:
                    pool.wait_ge(summed.sem, summed.after(g, e))
                    prev = acc
                nc.gpsimd.tensor_tensor(acc[:], prev[:], prod[:, e % 2], ALU.add).then_inc(summed.sem, 1)

            pool.wait_ge(const_pool, 6)
            for s in range(17):
                step(s, 0)
            for g in range(NG):
                if g:
                    finish(g - 1)
                for e in range(E):
                    if g + 1 < NG:
                        step(e, g + 1)
                    experts(g, e)
            finish(NG - 1)

        @block.vector
        def _(dve):
            class Chain:

                def __init__(self, sig):
                    self.sig, self.k = sig, 0

                def start(self, g):
                    assert self.k in (0, self.sig.per), self.k
                    self.g, self.k = g, 0

                def __call__(self, ins):
                    self.k += 1
                    ins.then_inc(self.sig.sem, 1)
                    dve.wait_ge(self.sig.sem, self.sig.after(self.g, self.k))

            ta, fin = Chain(ta_chain), Chain(fin_chain)

            def wide(ap):
                return ap.unsqueeze(2).broadcast_to([TOK, NJ, D])

            def widee(ap):
                return ap.unsqueeze(2).broadcast_to([TOK, NJ, E])

            def layernorm(link, src, cent, sqr, st, g, n, read=None):
                link(nc.vector.tensor_reduce(st[:, 0, :], src[:], AX.X, ALU.add))
                link(nc.vector.tensor_scalar(st[:, 1, :], st[:, 0, :], 1.0 / D, None, ALU.mult))
                link(nc.vector.tensor_tensor(cent[:], src[:], wide(st[:, 1, :]), ALU.subtract))
                link(nc.vector.tensor_tensor(sqr[:], cent[:], cent[:], ALU.mult))
                link(nc.vector.tensor_reduce(st[:, 2, :], sqr[:], AX.X, ALU.add))
                nc.vector.tensor_scalar(st[:, 2, :], st[:, 2, :], 1.0 / D, EPS, ALU.mult,
                                        ALU.add).then_inc(var_ready.sem, 1)
                dve.wait_ge(rstd_ready.sem, rstd_ready.after(g, n))

            dve.wait_ge(ld_tok, 16 * 18)
            nc.vector.scalar_tensor_tensor(out=core_abs[:], in0=core_col[:], scalar=-1.0, in1=core_col[:],
                                           op0=ALU.mult, op1=ALU.max).then_inc(const_dve, 1)
            dve.wait_ge(const_dve, 1)
            nc.vector.tensor_scalar(w_tok[:, 2, :], w_tok[:, 2, :], core_abs[:, 0:1], None,
                                    ALU.mult).then_inc(const_dve, 1)

            def setup_rest():
                dve.wait_ge(ld_band, 16)
                for k in range(4):
                    last = nc.vector.tensor_copy(conv_w[:, k, :], conv_block(k))
                last.then_inc(const_dve, 1)
                dve.wait_ge(set_pe, 1)
                nc.vector.tensor_copy(wo_t[:], pc[0:D, 0:D]).then_inc(const_dve, 1)
                nc.vector.tensor_copy(b1_col[:], pc[:, 128:128 + E]).then_inc(const_dve, 1)
                dve.wait_ge(zeroed, 5)
                dve.wait_ge(set_pe, 2)
                for b in range(PAIR):
                    r = slice(b * D, (b + 1) * D)
                    nc.vector.tensor_copy(w_qk[r, r], pd[r, 0:D])
                    last = nc.vector.tensor_copy(w_vo[r, r], pd[r, 128:128 + D])
                last.then_inc(const_dve, 1)
                dve.wait_ge(const_pool, 4)
                nc.vector.tensor_copy(row_cnt[:], row_pos[:]).then_inc(const_dve, 1)
                nc.vector.tensor_copy(prio[:, 0, :], prio_i[:]).then_inc(const_dve, 1)
                dve.wait_ge(const_dve, 8)
                nc.vector.tensor_scalar(row_cnt[:], row_cnt[:], 1.0, None, ALU.max).then_inc(const_dve, 1)
                dve.wait_ge(const_dve, 9)
                nc.vector.reciprocal(row_inv[:], row_cnt[:]).then_inc(const_dve, 1)
                dve.wait_ge(const_dve, 10)
                dve.wait_ge(ld_gate, 16 * 11)

            def split_w1():
                dve.wait_ge(w1_ready, 1)
                nc.vector.tensor_tensor(w1_lo[:], w1_raw[:], w1_hi[:].bitcast(F32),
                                        ALU.subtract).then_inc(w1_ready, 1)

            def step(s, g):
                if s == 0:
                    ta.start(g)
                    dve.wait_ge(x_turned.sem, x_turned.after(g, 2))
                    nc.vector.tensor_copy(x_t[:, halves[1]], pb[:, 0:HT]).then_inc(xt_dve.sem, 1)
                elif s == 2:
                    dve.wait_ge(tanh2.sem, tanh2.after(g, 1))
                    nc.vector.tensor_tensor(sq[:, halves[0]], act2[:, halves[0]], act2[:, halves[0]],
                                            ALU.mult).then_inc(squared_d.sem, 1)
                elif s == 4:
                    flat = bias_last[:].rearrange("p b d -> p (b d)").unsqueeze(1).broadcast_to([TOK, NR, P])
                    for h, ps in enumerate([pa, pb]):
                        dve.wait_ge(mm4.sem, mm4.after(g, h + 1))
                        nc.vector.tensor_tensor(pre4[:, NR * h:NR * (h + 1), :],
                                                ps[0:TOK, 0:NR * P].rearrange("p (c n) -> p c n", c=NR),
                                                flat, ALU.add).then_inc(biased4.sem, 1)
                elif s == 5:
                    dve.wait_ge(conv_done.sem, conv_done.after(g, 1))
                    ta(nc.vector.tensor_copy(hres[:].rearrange("p j d -> p (j d)"), pc[0:TOK, 0:NJ * D]))
                    layernorm(ta, hres, xc, xsq, stat, g, 1)
                    nc.vector.tensor_tensor(xn1[:], xc[:], wide(stat[:, 3, :]), ALU.mult).then_inc(ln1_done.sem, 1)
                elif s == 8:
                    dve.wait_ge(qv_done.sem, qv_done.after(g, 2))
                    nc.vector.tensor_copy(v_s[:].rearrange("p r n -> p (r n)"), pb[0:TOK, 0:NR * P]).then_inc(v_ready.sem, 1)
                elif s == 9:
                    for b, (p0, p1) in enumerate([(pa, pb), (pc, pd)]):
                        dve.wait_ge(logit_done.sem, logit_done.after(g, b + 1))
                        for o, src in ((TO, p1[0:TOK, 0:TOK]), (0, p0[0:TOK, 0:TOK]),
                                       (TO + 2 * TOK, p0[0:TOK, TO:TO + TOK])):
                            if o == 0:
                                dve.wait_ge(off_ready.sem, off_ready.after(g, 2 * b + 1))
                            nc.vector.scalar_tensor_tensor(out=attn[:, b, o:o + TOK], in0=src, scalar=0.0,
                                                           in1=causal_cap[:], op0=ALU.max,
                                                           op1=ALU.min).then_inc(diag_ready.sem, 1)
                elif s == 10:
                    dve.wait_ge(ctx_done.sem, ctx_done.after(g, 1))
                    for r in range(NR):
                        js = slice(PAIR * r, PAIR * (r + 1))
                        ins = nc.vector.scalar_tensor_tensor(
                            out=h2[:, js, :].rearrange("p j d -> p (j d)"), in0=pa[0:TOK, r * P:(r + 1) * P],
                            scalar=row_inv[:, r:r + 1], in1=hres[:, js, :].rearrange("p j d -> p (j d)"),
                            op0=ALU.mult, op1=ALU.add)
                    ta(ins)
                    layernorm(ta, h2, xc, xsq, stat, g, 2)
                    ta(nc.vector.tensor_tensor(xn2[:], xc[:], wide(stat[:, 3, :]), ALU.mult))
                    ta(nc.vector.tensor_copy(split[:, :, 0, :], xn2[:]))
                    nc.vector.tensor_tensor(split[:, :, 1, :], xn2[:], split[:, :, 0, :].bitcast(F32),
                                            ALU.subtract).then_inc(ln2_done.sem, 1)
                elif s == 12:
                    dve.wait_ge(split_turned.sem, split_turned.after(g, 2))
                    nc.vector.tensor_copy(xg[:, 1, 0:TO], pc[:, 0:TO]).then_inc(xg_dve.sem, 1)
                elif s == 13:
                    first, second = top[:, 0, :], top[:, 1, :]
                    dve.wait_ge(gate_done.sem, gate_done.after(g, 1))
                    pr = prio[:].broadcast_to([TOK, NJ, E])
                    ta(nc.vector.tensor_tensor(logits[:], pd[0:TOK, 0:NJ * E].rearrange("p (j e) -> p j e", e=E),
                                               gate_bb[:].broadcast_to([TOK, NJ, E]), ALU.add))

                    def pick(values, best, chosen):
                        ta(nc.vector.tensor_reduce(best, values, AX.X, ALU.max))
                        ta(nc.vector.tensor_tensor(work[:, 0], values, widee(best), ALU.is_equal))
                        ta(nc.vector.tensor_tensor(work[:, 1], work[:, 0], pr, ALU.mult))
                        ta(nc.vector.tensor_reduce(top[:, 4, :], work[:, 1], AX.X, ALU.max))
                        return nc.vector.tensor_tensor(chosen, work[:, 1], widee(top[:, 4, :]), ALU.is_equal)

                    ta(pick(logits[:], first, pick1[:]))
                    ta(nc.vector.scalar_tensor_tensor(out=work[:, 2], in0=pick1[:], scalar=-BIG, in1=logits[:],
                                                      op0=ALU.mult, op1=ALU.add))
                    pending = pick(work[:, 2], second, pick2[:])
                    ta(pending)
                    nc.vector.tensor_tensor(top[:, 2, :], second, first, ALU.subtract).then_inc(diff_ready.sem, 1)
                elif s == 14:
                    dve.wait_ge(exp_ready.sem, exp_ready.after(g, 1))
                    ta(nc.vector.tensor_scalar(top[:, 5, :], top[:, 3, :], 1.0, None, ALU.add))
                    ta(nc.vector.reciprocal(top[:, 6, :], top[:, 5, :]))
                    ta(nc.vector.tensor_tensor(top[:, 7, :], top[:, 3, :], top[:, 6, :], ALU.mult))
                    ta(nc.vector.tensor_tensor(work[:, 0], pick1[:], widee(top[:, 6, :]), ALU.mult))
                    ta(nc.vector.tensor_tensor(work[:, 1], pick2[:], widee(top[:, 7, :]), ALU.mult))
                    nc.vector.tensor_tensor(gates_new[:], work[:, 0], work[:, 1], ALU.add).then_inc(gates_made.sem, 1)
                elif s == 16:
                    dve.wait_ge(b2_done.sem, b2_done.after(g, 1))
                    nc.vector.tensor_tensor(y_base[:].rearrange("p j d -> p (j d)"), pb[0:TOK, 0:NJ * D],
                                            xn2[:].rearrange("p j d -> p (j d)"), ALU.add).then_inc(y_base_ready.sem, 1)

            def hand_over(g):
                if g:
                    dve.wait_ge(z_done.sem, z_done.after(g - 1, PAIR * E))
                dve.wait_ge(xg_act.sem, xg_act.after(g, 1))
                dve.wait_ge(xg_dve.sem, xg_dve.after(g, 1))
                nc.vector.tensor_copy(xs[:], xg[:]).then_inc(handed.sem, 1)

            def hand_over_late(g):
                dve.wait_ge(gates_made.sem, gates_made.after(g, 1))
                if g:
                    dve.wait_ge(gated.sem, gated.after(g - 1, E))
                nc.vector.tensor_copy(gates[:], gates_new[:]).then_inc(handed.sem, 1)

            def experts(g, e):
                dve.wait_ge(y_done.sem, y_done.after(g, e + 1))
                if g or e >= 2:
                    dve.wait_ge(summed.sem, summed.after(g, max(e - 1, 0)))
                if e == 0:
                    dve.wait_ge(handed.sem, handed.after(g, 2))
                nc.vector.tensor_tensor(prod[:, e % 2], y[e % 2][0:TOK, 0:NJ * D].rearrange("p (j d) -> p j d", d=D),
                                        gates[:, :, e:e + 1].broadcast_to([TOK, NJ, D]),
                                        ALU.mult).then_inc(gated.sem, 1)

            def finish(g):
                fin.start(g)
                dve.wait_ge(summed.sem, summed.after(g, E))
                link = fin
                link(nc.vector.tensor_reduce(ystat[:, 0, :], acc[:], AX.X, ALU.add))
                link(nc.vector.tensor_scalar(ystat[:, 1, :], ystat[:, 0, :], 1.0 / D, None, ALU.mult))
                nc.vector.tensor_tensor(yc[:], acc[:], wide(ystat[:, 1, :]), ALU.subtract).then_inc(acc_read.sem, 1)
                dve.wait_ge(acc_read.sem, acc_read.after(g, 1))
                link(nc.vector.tensor_tensor(ysq[:], yc[:], yc[:], ALU.mult))
                link(nc.vector.tensor_reduce(ystat[:, 2, :], ysq[:], AX.X, ALU.add))
                nc.vector.tensor_scalar(ystat[:, 2, :], ystat[:, 2, :], 1.0 / D, EPS, ALU.mult,
                                        ALU.add).then_inc(yvar_ready.sem, 1)
                dve.wait_ge(yrstd_ready.sem, yrstd_ready.after(g, 1))
                link(nc.vector.tensor_tensor(yn[:], yc[:], wide(ystat[:, 3, :]), ALU.mult))
                link(nc.vector.tensor_tensor(yn[:], yn[:], gamma_b[:].broadcast_to([TOK, NJ, D]), ALU.mult))
                link(nc.vector.tensor_tensor(yn[:], yn[:], beta_b[:].broadcast_to([TOK, NJ, D]), ALU.add))
                if g:
                    dve.wait_ge(stored.sem, stored.after(g - 1, PAIR))
                nc.vector.tensor_tensor(y_out[:], yn[:], h2_m[:], ALU.add).then_inc(y_out_ready.sem, 1)

            setup_rest()
            for s in range(17):
                step(s, 0)
                if s == 9:
                    split_w1()
            for g in range(NG):
                hand_over(g)
                hand_over_late(g)
                if g:
                    finish(g - 1)
                    dve.wait_ge(y_out_ready.sem, y_out_ready.after(g - 1, 1))
                nc.vector.tensor_copy(h2_m[:], h2[:]).then_inc(handed.sem, 1)
                dve.wait_ge(handed.sem, handed.after(g, 3))
                for e in range(E):
                    if e:
                        experts(g, e - 1)
                    if g + 1 < NG:
                        step(e, g + 1)
                experts(g, E - 1)
                if g + 1 < NG:
                    step(16, g + 1)
            finish(NG - 1)

        @block.tensor
        def _(pe):
            mm = nc.tensor.matmul

            def setup_products():
                pe.wait_ge(const_pool, 1)
                pe.wait_ge(ld_attn, 16 * 7)
                nc.tensor.transpose(pc[0:D, 0:D], wo_s[:], ident[0:D, 0:D])
                nc.tensor.transpose(pc[:, 128:128 + E], b1_s[:], ident[0:E, 0:E]).then_inc(set_pe, 1)
                pe.wait_ge(const_dve, 4)
                mm(pd[:, 0:D], wq2[:].rearrange("p b d -> p (b d)"), wk_s[:], start=True, stop=True)
                mm(pd[:, 128:128 + D], wv2[:].rearrange("p b d -> p (b d)"), wo_t[:],
                   start=True, stop=True).then_inc(set_pe, 1)

            def step(s, g):
                if s == 0:
                    pe.wait_ge(x_in_ready.sem, x_in_ready.after(g, PAIR))
                    if g:
                        pe.wait_ge(y_base_ready.sem, y_base_ready.after(g - 1, 1))
                    for c in range(NT):
                        ins = nc.tensor.transpose((pa, pb)[c // NR][:, c % NR * TOK:(c % NR + 1) * TOK],
                                                  x_in[:, c].rearrange("p b d -> p (b d)"), ident[0:TOK, 0:TOK])
                        if c % NR == NR - 1:
                            ins.then_inc(x_turned.sem, 1)
                elif s in (1, 2, 3):
                    dst, src, said = {1: ((pc, pd), x_t, mm1), 2: ((pa, pb), act1, mm2), 3: ((pc, pd), sq, mm3)}[s]
                    for h in range(2):
                        ready = {1: (xt_act, xt_dve), 2: (tanh1, tanh1), 3: (squared_d, squared_p)}[s][h]
                        pe.wait_ge(ready.sem, ready.after(g, h + 1 if s == 2 else 1))
                        mm(dst[h][:, 0:HT], w_tok[:, s - 1, :], src[:, halves[h]],
                           start=True, stop=True).then_inc(said.sem, 1)
                elif s == 4:
                    for c in range(NT):
                        if c % NR == 0:
                            pe.wait_ge(tanh3.sem, tanh3.after(g, c // NR + 1))
                        ins = mm((pa, pb)[c // NR][0:TOK, c % NR * P:(c % NR + 1) * P],
                                 act3[:, c * TOK:(c + 1) * TOK], w_tok[:, 3, :], start=True, stop=True)
                        if c % NR == NR - 1:
                            ins.then_inc(mm4.sem, 1)
                elif s == 5:
                    pe.wait_ge(tanh4.sem, tanh4.after(g, 1))
                    for r in range(NR):
                        cs = [c for c in range(2 * r - 1, 2 * r + 3) if 0 <= c < NT]
                        for c in cs:
                            ins = mm(pc[0:TOK, r * P:(r + 1) * P], conv_w[:, c - 2 * r + 1, :], act4[:, c, :],
                                     start=c == cs[0], stop=c == cs[-1])
                    ins.then_inc(conv_done.sem, 1)
                elif s == 7:
                    pe.wait_ge(ln1_done.sem, ln1_done.after(g, 1))
                    for r in range(NR):
                        ins = nc.tensor.transpose(pd[:, r * TOK:(r + 1) * TOK],
                                                  xn1[:, PAIR * r:PAIR * (r + 1)].rearrange("p b d -> p (b d)"),
                                                  ident[0:TOK, 0:TOK])
                    ins.then_inc(xn1_turned.sem, 1)
                elif s == 8:
                    pe.wait_ge(xn1t_ready.sem, xn1t_ready.after(g, 1))
                    mm(pa[:, 0:TO], w_qk[:], xn1_t[:], start=True, stop=True).then_inc(qv_done.sem, 1)
                    for r in range(NR):
                        ins = mm(pb[0:TOK, r * P:(r + 1) * P], xn1_t[:, r * TOK:(r + 1) * TOK], w_vo[:],
                                 start=True, stop=True)
                    ins.then_inc(qv_done.sem, 1)
                elif s == 9:
                    pe.wait_ge(qt_ready.sem, qt_ready.after(g, 1))
                    pe.wait_ge(v_ready.sem, v_ready.after(g, 1))
                    for b, (p0, p1) in enumerate([(pa, pb), (pc, pd)]):
                        f = slice(b * D, (b + 1) * D)
                        for m, dst in ((0, p0[0:TOK, 0:TO]), (1, p1[0:TOK, 0:2 * TOK]), (2, p0[0:TOK, TO:TO + TOK])):
                            ins = mm(dst, xn1_t[f, m * TOK:(m + 1) * TOK], q_t[f, m * TOK:TO], start=True, stop=True)
                        ins.then_inc(logit_done.sem, 1)
                elif s == 10:
                    pe.wait_ge(off_ready.sem, off_ready.after(g, 2 * PAIR))
                    pe.wait_ge(diag_ready.sem, diag_ready.after(g, NR * PAIR))
                    at = [0, TO, TO + 2 * TOK]
                    for r in range(NR):
                        for b in range(PAIR):
                            for m in range(r + 1):
                                ins = mm(pa[0:TOK, r * P + b * D:r * P + (b + 1) * D],
                                         attn[:, b, at[m] + (r - m) * TOK:at[m] + (r - m + 1) * TOK],
                                         v_s[:, m, b * D:(b + 1) * D], start=m == 0, stop=m == r)
                    ins.then_inc(ctx_done.sem, 1)
                elif s == 12:
                    pe.wait_ge(ln2_done.sem, ln2_done.after(g, 1))
                    for b in range(PAIR):
                        for r in range(NR):
                            ins = nc.tensor.transpose(
                                (pb, pc)[b][:, r * TOK:(r + 1) * TOK],
                                split[:, PAIR * r + b].rearrange("p s d -> p (s d)").bitcast(F32),
                                ident[0:TOK, 0:TOK])
                        ins.then_inc(split_turned.sem, 1)
                elif s == 13:
                    pe.wait_ge(xg_act.sem, xg_act.after(g, 1))
                    pe.wait_ge(xg_dve.sem, xg_dve.after(g, 1))
                    for j in range(NJ):
                        r, b = j // PAIR, j % PAIR
                        ins = mm(pd[0:TOK, j * E:(j + 1) * E], xg[:, b, r * TOK:(r + 1) * TOK].bitcast(F32),
                                 gate_w2[:], start=True, stop=True)
                    ins.then_inc(gate_done.sem, 1)
                elif s == 15:
                    pe.wait_ge(gates_made.sem, gates_made.after(g, 1))
                    nc.tensor.transpose(pa[0:NJ * E, 0:TOK], gates_new[:].rearrange("p j e -> p (j e)"),
                                        ident[0:TOK, 0:TOK]).then_inc(gates_turned.sem, 1)
                elif s == 16:
                    pe.wait_ge(gates_t_ready.sem, gates_t_ready.after(g, 1))
                    mm(pb[0:TOK, 0:NJ * D], gates_t[:], b2_diag[:].rearrange("p j d -> p (j d)"),
                       start=True, stop=True).then_inc(b2_done.sem, 1)

            def expert_in(g, e):
                if e == 0:
                    pe.wait_ge(handed.sem, handed.after(g, 1) if g == 0 else 3 * g + 1)
                for b in range(PAIR):
                    if g or e:
                        n = PAIR * (e - 1) + b + 1 if e else 0
                        pe.wait_ge(relu_done.sem, relu_done.after(g, n))
                    mm(z[b][:, 0:W], w1_hi[:, e, :], xs[:, b, :], start=True, stop=False)
                    mm(z[b][:, 0:W], w1_lo[:, e, :], xs[:, b, :], start=False, stop=True).then_inc(z_done.sem, 1)

            def expert_out(g, e):
                pe.wait_ge(relu_done.sem, relu_done.after(g, PAIR * (e + 1)))
                if g or e >= 2:
                    pe.wait_ge(gated.sem, gated.after(g, max(e - 1, 0)))
                for j in range(NJ):
                    r, b = j // PAIR, j % PAIR
                    ins = mm(y[e % 2][0:TOK, j * D:(j + 1) * D], hid[:, e % 2, b, r * TOK:(r + 1) * TOK],
                             w2_s[:, e, :], start=True, stop=True)
                ins.then_inc(y_done.sem, 1)

            setup_products()
            pe.wait_ge(ld_tok, 16 * 18)
            pe.wait_ge(const_dve, 10)
            pe.wait_ge(ld_gate, 16 * 11)
            for s in range(17):
                step(s, 0)
            pe.wait_ge(w1_ready, 2)
            pe.wait_ge(ld_w2, 16)
            for g in range(NG):
                for e in range(E):
                    expert_in(g, e)
                    if g + 1 < NG:
                        step(e, g + 1)
                    if e:
                        expert_out(g, e - 1)
                expert_out(g, E - 1)
                if g + 1 < NG:
                    step(16, g + 1)


_INS = ["x", "L0_tok_W_in", "L0_tok_b_in", "L0_tok_W_out", "L0_tok_b_out", "L0_tok_core_diag", "L0_tok_conv_filter",
        "L0_attn_Wq", "L0_attn_Wk", "L0_attn_Wv", "L0_attn_Wo", "L0_ffn_gate_w", "L0_ffn_gate_b", "L0_ffn_w1",
        "L0_ffn_b1", "L0_ffn_w2", "L0_ffn_b2", "L0_ffn_gamma", "L0_ffn_beta"]
_OUT = ((8, 375, 64), "float32")


def kernel(**inputs):
    import numpy as _np
    import concourse.bacc as _bacc
    from concourse import mybir as _mybir
    from concourse.bass_utils import run_bass_kernel_spmd as _run

    nc = _bacc.Bacc("TRN2", target_bir_lowering=False, num_devices=1)
    arrays, args = {}, []
    for name in _INS:
        a = _np.ascontiguousarray(inputs[name])
        arrays[f"in_{name}_dram"] = a
        args.append(nc.dram_tensor(f"in_{name}_dram", a.shape, _mybir.dt.from_np(a.dtype), kind="ExternalInput").ap())
    args.append(nc.dram_tensor("out_dram", _OUT[0], _mybir.dt.from_np(_np.dtype(_OUT[1])), kind="ExternalOutput").ap())
    audio_tower(nc, *args)
    r = _run(nc, [arrays], core_ids=[0])
    return r.results[0]["out_dram"]
```

```python
from contextlib import ExitStack

import concourse.bass as bass
from concourse import mybir

F32 = mybir.dt.float32
F32R = mybir.dt.float32r
I32 = mybir.dt.int32
ALU = mybir.AluOpType
ACT = mybir.ActivationFunctionType
AX = mybir.AxisListType

P = 128
TOK = 125
PAIR = 2
LAG = 2
HID = 3
GE = 2
ROW = 768
BIG = 3.0e38
EPS = 1e-5


class Signal:

    def __init__(self, sem, per, unit=1):
        self.sem, self.per, self.unit = sem, per, unit

    def after(self, g, k):
        return (self.per * g + k) * self.unit


def audio_tower(nc, x, w_in, b_in, w_out, b_out, core, filt, wq, wk, wv, wo,
                gate_w, gate_b, w1, b1, w2, b2, gamma, beta, out):
    B, T, D = x.shape
    TO = out.shape[1]
    E, _, F = w1.shape
    NG = B // PAIR
    NT = T // TOK
    NR = TO // TOK
    NJ = NR * PAIR
    HT = T // 2
    W = TO + 1
    TAPS = filt.shape[0]
    assert D * PAIR == P and F == P and T == 2 * TO and HT == NR * TOK

    ctx = ExitStack()
    with ctx:
        def sb(name, shape, dt=F32):
            return ctx.enter_context(nc.sbuf_tensor(name, shape, dt))

        def bank(name):
            return ctx.enter_context(nc.psum_tensor(name, [P, 512], F32))

        def sem(name):
            return ctx.enter_context(nc.semaphore(name))

        def signal(name, per=1, unit=1):
            return Signal(sem(name), per, unit)

        ident = sb("ident", [P, P])
        w_tok = sb("w_tok", [P, 4, P])
        bias_tok = sb("bias_tok", [P, 3])
        bias_last = sb("bias_last", [TOK, PAIR, D])
        core_col = sb("core_col", [P, 1])
        core_abs = sb("core_abs", [P, 1])
        filt_row = sb("filt_row", [1, ROW])
        filt_pad = nc.dram_tensor("filt_pad", [1, ROW], F32)
        band = sb("band", [TOK, 640])
        conv_w = sb("conv_w", [TOK, 4, TOK])
        wq2 = sb("wq2", [D, PAIR, D])
        wk_s = sb("wk_s", [D, D])
        wv2 = sb("wv2", [D, PAIR, D])
        wo_s = sb("wo_s", [D, D])
        wo_t = sb("wo_t", [D, D])
        w_qk = sb("w_qk", [P, P])
        w_vo = sb("w_vo", [P, P])
        minus_half = sb("minus_half", [TOK, NJ])
        causal_cap = sb("causal_cap", [TOK, TOK])
        row_pos = sb("row_pos", [TOK, NR], I32)
        row_cnt = sb("row_cnt", [TOK, NR])
        row_inv = sb("row_inv", [TOK, NR])
        prio_i = sb("prio_i", [TOK, E], I32)
        prio = sb("prio", [TOK, 1, E])
        gate_raw = sb("gate_raw", [P, E])
        gate_s = sb("gate_s", [P, 2, E], F32R)
        gate_bb = sb("gate_bb", [TOK, 1, E])
        w1_raw = sb("w1_raw", [P, E, F])
        w1_hi = sb("w1_hi", [P, E, F], F32R)
        w1_lo = sb("w1_lo", [P, E, F], F32R)
        w2_s = sb("w2_s", [F, E, D])
        b1_s = sb("b1_s", [E, F])
        b1_col = sb("b1_col", [F, E])
        b1_neg = sb("b1_neg", [F, E])
        w2b1 = sb("w2b1", [D, NR, PAIR, E])
        b2_diag = sb("b2_diag", [NJ * E, NJ, D])
        gamma_b = sb("gamma_b", [TOK, 1, D])
        beta_b = sb("beta_b", [TOK, 1, D])

        x_in = [sb(f"x_in{i}", [TOK, NT, PAIR, D]) for i in range(2)]
        x_t = [sb(f"x_t{i}", [P, T]) for i in range(2)]
        act1 = [sb(f"act1_{i}", [P, T]) for i in range(2)]
        act2 = [sb(f"act2_{i}", [P, T]) for i in range(2)]
        sq = [sb(f"sq{i}", [P, T]) for i in range(2)]
        act3 = [sb(f"act3_{i}", [P, T]) for i in range(2)]
        pre4 = [sb(f"pre4_{i}", [TOK, NT, P]) for i in range(2)]
        act4 = [sb(f"act4_{i}", [TOK, NT, P]) for i in range(2)]
        hres = [sb(f"hres{i}", [TOK, NJ, D]) for i in range(2)]
        xn1 = [sb(f"xn1_{i}", [TOK, NJ, D]) for i in range(2)]
        xn1_t = sb("xn1_t", [P, TO])
        q_t = sb("q_t", [P, TO])
        v_s = sb("v_s", [TOK, NR, P])
        attn = sb("attn", [TOK, PAIR, NJ * TOK])
        h2 = [sb(f"h2_{i}", [TOK, NJ, D]) for i in range(3)]
        xn2 = sb("xn2", [TOK, NJ, D])
        split = sb("split", [TOK, NJ, 2, D], F32R)
        xs = [sb(f"xs{i}", [P, PAIR, W], F32R) for i in range(2)]
        logits = sb("logits", [TOK, NJ, E])
        top = sb("top", [TOK, 8, NJ])
        pick1 = sb("pick1", [TOK, NJ, E])
        pick2 = sb("pick2", [TOK, NJ, E])
        work = sb("work", [TOK, 4, NJ, E])
        gates = sb("gates", [TOK, NJ, E])
        gates_t = sb("gates_t", [NJ * E, TOK])
        y_base = [sb(f"y_base{i}", [TOK, NJ, D]) for i in range(2)]
        gates_dram = nc.dram_tensor("gates_dram", [NG, E, PAIR, TO], F32)
        gate_all = sb("gate_all", [P, E, PAIR, TO])
        hid = sb("hid", [F, HID, PAIR, TO])
        rel = sb("rel", [F, 2, TO])
        y_t = sb("y_t", [P, TO])
        y_tok = sb("y_tok", [TOK, NJ, D])
        yn = sb("yn", [TOK, NJ, D])
        y_out = sb("y_out", [TOK, NJ, D])
        cent = {k: sb(f"cent_{k}", [TOK, NJ, D]) for k in "TAF"}
        csq = {k: sb(f"csq_{k}", [TOK, NJ, D]) for k in "TAF"}
        stat = {k: sb(f"stat_{k}", [TOK, 3, NJ]) for k in "TAF"}

        z = [bank("z0"), bank("z1")]
        y = [bank("y0"), bank("y1")]
        t_banks = [bank("t0"), bank("t1")]
        a0, a1 = bank("a0"), bank("a1")

        def banks_of(g):
            return z if g == 1 else t_banks

        ld_tok = sem("ld_tok")
        ld_filt = sem("ld_filt")
        ld_band = sem("ld_band")
        ld_attn = sem("ld_attn")
        ld_gate = sem("ld_gate")
        ld_w1 = sem("ld_w1")
        ld_w2 = sem("ld_w2")
        zeroed = sem("zeroed")
        const_pool = sem("const_pool")
        pool_chain = sem("pool_chain")
        const_dve = sem("const_dve")
        set_pe = sem("set_pe")
        w1_ready = sem("w1_ready")
        x_in_ready = [sem(f"x_in_ready{i}") for i in range(2)]
        x_turned = signal("x_turned", 2)
        xt_ready = signal("xt_ready", 2)
        mm1 = signal("mm1", 2)
        tanh1 = signal("tanh1", 2)
        mm2 = signal("mm2", 2)
        tanh2 = signal("tanh2", 2)
        squared = signal("squared", 2)
        mm3 = signal("mm3", 2)
        tanh3 = signal("tanh3", 2)
        mm4 = signal("mm4", 2)
        biased4 = signal("biased4", 2)
        tanh4 = signal("tanh4", 2)
        conv_done = signal("conv_done")
        hres_ready = signal("hres_ready")
        ln_cent = {k: signal(f"ln_cent_{k}") for k in "TAF"}
        ln_sq = {k: signal(f"ln_sq_{k}") for k in "TAF"}
        ln_var = {k: signal(f"ln_var_{k}") for k in "TAF"}
        ln_rstd = {k: signal(f"ln_rstd_{k}") for k in "TAF"}
        ln_done = {k: signal(f"ln_done_{k}") for k in "TAF"}
        xn1_turned = signal("xn1_turned")
        xn1t_ready = signal("xn1t_ready")
        qv_done = signal("qv_done", 2)
        qt_ready = signal("qt_ready")
        v_ready = signal("v_ready")
        logit_done = signal("logit_done", PAIR)
        off_ready = signal("off_ready", 2 * PAIR)
        diag_ready = signal("diag_ready", NR * PAIR)
        ctx_done = signal("ctx_done")
        split_ready = signal("split_ready")
        split_turned = signal("split_turned", PAIR)
        xs_ready = signal("xs_ready", PAIR)
        gate_done = signal("gate_done")
        diff_ready = signal("diff_ready")
        exp_ready = signal("exp_ready")
        gates_made = signal("gates_made")
        gates_turned = signal("gates_turned")
        gates_t_ready = signal("gates_t_ready")
        gates_out = signal("gates_out", NR, 16)
        gate_all_ready = [signal(f"gate_all_ready{k}", 1, 16) for k in range(E // GE)]
        b2_done = signal("b2_done")
        y_base_ready = signal("y_base_ready")
        z_done = signal("z_done", PAIR * E)
        hid0_ready = signal("hid0_ready", E)
        rel_ready = signal("rel_ready", E)
        hid1_ready = signal("hid1_ready", E)
        y_added = signal("y_added", E)
        yt_ready = signal("yt_ready")
        y_turned = signal("y_turned")
        y_scaled = signal("y_scaled", 2)
        y_out_ready = signal("y_out_ready")
        stored = signal("stored", PAIR, 16)
        t_chain = signal("t_chain", 2)
        a_chain = signal("a_chain", 22)
        f_chain = signal("f_chain", 3)

        beside = {0: [("T", 2, 0)], 1: [("A", 1, 0), ("T", 2, 1)], 2: [("A", 1, 1), ("F", -1, 0)],
                  3: [("A", 1, 2), ("F", -1, 1), ("T", 2, 2)], 4: [("A", 1, 3), ("F", -1, 2)],
                  5: [("A", 1, 4), ("F", -1, 3)], 6: [("A", 1, 5), ("T", 2, 3)], 7: [("A", 1, 6), ("F", -1, 4)],
                  8: [("A", 1, 7), ("T", 2, 4)], 9: [("A", 1, 8)], 10: [("A", 1, 9)],
                  11: [("A", 1, 10), ("T", 2, 5)], 12: [("A", 1, 11), ("T", 2, 6)],
                  13: [("A", 1, 12), ("T", 2, 7)], 14: [("A", 1, 13), ("T", 2, 8)], 15: []}
        plan = [("T", 0, 0), ("T", 0, 1), ("T", 1, 0), ("T", 0, 2), ("T", 1, 1), ("T", 0, 3), ("T", 1, 2),
                ("T", 0, 4), ("T", 1, 3), ("T", 0, 5), ("T", 0, 6), ("T", 0, 7), ("T", 0, 8), ("A", 0, 0),
                ("T", 1, 4), ("A", 0, 1), ("A", 0, 2), ("A", 0, 3), ("A", 0, 4), ("T", 1, 5), ("A", 0, 5),
                ("A", 0, 6), ("A", 0, 7), ("A", 0, 8), ("A", 0, 9), ("A", 0, 10), ("A", 0, 11), ("T", 1, 6),
                ("A", 0, 12), ("T", 1, 7), ("A", 0, 13), ("T", 1, 8)]
        for n in range(NG * E + LAG):
            g, e = n // E, n % E
            if n < NG * E:
                plan.append(("in", g, e))
                plan += [(k, g + d, s) for k, d, s in beside[e] if 0 <= g + d < NG]
            if n >= LAG:
                plan.append(("out", (n - LAG) // E, (n - LAG) % E))
        plan += [("F", NG - 1, s) for s in range(5)]

        def walk(stages):
            for kind, g, s in plan:
                if kind in stages:
                    stages[kind](g, s)

        block = ctx.enter_context(nc.Block())
        halves = [slice(0, HT), slice(HT, T)]
        MID = 368
        BANDW = MID + TAPS // 2 + 2 * TOK + 1
        assert BANDW + TOK <= ROW and MID + TAPS // 2 >= 3 * TOK

        def conv_block(k):
            top_col = MID + TAPS // 2 + TOK * (k - 1)
            return band[:, top_col:top_col - 2 * TOK:-2]

        @block.sync
        def _(sp):
            def load_x(g):
                for b in range(PAIR):
                    src = x[PAIR * g + b].rearrange("(c p) d -> p c d", p=TOK)
                    sp.dma_start(x_in[g % 2][:, :, b, :], src).then_inc(x_in_ready[g % 2], 16)

            def stage_a(g, s):
                if s == 12:
                    sp.wait_ge(gates_t_ready.sem, gates_t_ready.after(g, 1))
                    rows = gates_dram[g].rearrange("e b (r p) -> r b e p", r=NR)
                    for r in range(NR):
                        sp.dma_start(rows[r], gates_t[r * PAIR * E:(r + 1) * PAIR * E, :]).then_inc(gates_out.sem, 16)
                    sp.wait_ge(gates_out.sem, gates_out.after(g, NR))
                    for k in range(E // GE):
                        if g:
                            sp.wait_ge(hid0_ready.sem, hid0_ready.after(g - 1, GE * (k + 1)))
                            sp.wait_ge(hid1_ready.sem, hid1_ready.after(g - 1, GE * (k + 1)))
                        src = gates_dram[g, GE * k:GE * (k + 1)].rearrange("e b t -> (e b t)")
                        sp.dma_start(gate_all[:, GE * k:GE * (k + 1)].rearrange("p e b t -> p (e b t)"),
                                     src.partition_broadcast(P)).then_inc(gate_all_ready[k].sem, 16)

            def stage_f(g, s):
                if s == 4:
                    sp.wait_ge(y_out_ready.sem, y_out_ready.after(g, 1))
                    view = y_out[:].rearrange("p (r b) d -> p r b d", b=PAIR)
                    for b in range(PAIR):
                        dst = out[PAIR * g + b].rearrange("(r p) d -> p r d", p=TOK)
                        sp.dma_start(dst, view[:, :, b, :]).then_inc(stored.sem, 16)

            def stage_t(g, s):
                if s == 1 and g + 2 < NG:
                    sp.wait_ge(x_turned.sem, x_turned.after(g, 2))
                    load_x(g + 2)

            load_x(0)
            sp.wait_ge(zeroed, 1)
            layers = [w_in[0], w_in[1], w_out[1], w_out[0]]
            for n, w in enumerate(layers):
                for b in range(PAIR):
                    sp.dma_start(w_tok[b * D:(b + 1) * D, n, b * D:(b + 1) * D], w).then_inc(ld_tok, 16)
            load_x(1)
            sp.dma_start(w2_s[:], w2.rearrange("e f h -> f e h")).then_inc(ld_w2, 16)
            sp.wait_ge(zeroed, 3)
            for j in range(NJ):
                sp.dma_start(b2_diag[j * E:(j + 1) * E, j, :], b2).then_inc(ld_gate, 16)
            for b in range(PAIR):
                sp.dma_start(gate_raw[b * D:(b + 1) * D, :], gate_w).then_inc(ld_gate, 16)
            sp.dma_start(gate_bb[:, 0, :], gate_b.partition_broadcast(TOK)).then_inc(ld_gate, 16)
            sp.dma_start(gamma_b[:, 0, :], gamma.partition_broadcast(TOK)).then_inc(ld_gate, 16)
            sp.dma_start(beta_b[:, 0, :], beta.partition_broadcast(TOK)).then_inc(ld_gate, 16)
            walk({"T": stage_t, "A": stage_a, "F": stage_f})
            sp.wait_ge(stored.sem, stored.after(NG - 1, PAIR))

        @block.scalar
        def _(act):
            for n, bv in enumerate([b_in[0], b_in[1], b_out[1]]):
                for b in range(PAIR):
                    act.dma_start(bias_tok[b * D:(b + 1) * D, n:n + 1], bv.unsqueeze(1)).then_inc(ld_tok, 16)
            for b in range(PAIR):
                act.dma_start(bias_last[:, b, :], b_out[0].partition_broadcast(TOK)).then_inc(ld_tok, 16)
                act.dma_start(core_col[b * D:(b + 1) * D, :], core.unsqueeze(1)).then_inc(ld_tok, 16)
                act.dma_start(wq2[:, b, :], wq).then_inc(ld_attn, 16)
                act.dma_start(wv2[:, b, :], wv).then_inc(ld_attn, 16)
            act.dma_start(wk_s[:], wk).then_inc(ld_attn, 16)
            act.dma_start(wo_s[:], wo).then_inc(ld_attn, 16)
            act.dma_start(b1_s[:], b1).then_inc(ld_attn, 16)
            for b in range(PAIR):
                act.dma_start(w1_raw[b * D:(b + 1) * D, :, :], w1.rearrange("e h f -> h e f")).then_inc(ld_w1, 16)

            def square(k, g):
                act.wait_ge(ln_cent[k].sem, ln_cent[k].after(g, 1))
                act.activation(csq[k][:], cent[k][:], ACT.Square).then_inc(ln_sq[k].sem, 1)

            def stage_t(g, s):
                p, banks = g % 2, banks_of(g)
                if s == 0:
                    for h in range(2):
                        act.wait_ge(x_turned.sem, x_turned.after(g, h + 1))
                        act.copy(x_t[p][:, halves[h]], banks[h][:, 0:HT]).then_inc(xt_ready.sem, 1)
                elif s in (1, 2, 3):
                    done, dst, said = {1: (mm1, act1, tanh1), 2: (mm2, act2, tanh2), 3: (mm3, act3, tanh3)}[s]
                    for h in range(2):
                        act.wait_ge(done.sem, done.after(g, h + 1))
                        act.activation(dst[p][:, halves[h]], banks[h][:, 0:HT], ACT.Tanh,
                                       bias=bias_tok[:, s - 1:s]).then_inc(said.sem, 1)
                    if s == 2:
                        for h in range(2):
                            act.wait_ge(tanh2.sem, tanh2.after(g, h + 1))
                            act.activation(sq[p][:, halves[h]], act2[p][:, halves[h]],
                                           ACT.Square).then_inc(squared.sem, 1)
                elif s == 4:
                    for h in range(2):
                        cs = slice(NR * h, NR * (h + 1))
                        act.wait_ge(biased4.sem, biased4.after(g, h + 1))
                        act.activation(act4[p][:, cs], pre4[p][:, cs], ACT.Tanh).then_inc(tanh4.sem, 1)
                elif s == 5:
                    act.wait_ge(conv_done.sem, conv_done.after(g, 1))
                    act.copy(hres[p][:].rearrange("p j d -> p (j d)"),
                             banks[0][0:TOK, 0:NJ * D]).then_inc(hres_ready.sem, 1)
                elif s == 6:
                    square("T", g)

            def stage_a(g, s):
                if s == 0:
                    act.wait_ge(xn1_turned.sem, xn1_turned.after(g, 1))
                    act.copy(xn1_t[:], a0[:, 0:TO]).then_inc(xn1t_ready.sem, 1)
                elif s == 1:
                    act.wait_ge(qv_done.sem, qv_done.after(g, 1))
                    act.copy(q_t[:], a0[:, 0:TO]).then_inc(qt_ready.sem, 1)
                    act.wait_ge(qv_done.sem, qv_done.after(g, 2))
                    act.copy(v_s[:].rearrange("p r n -> p (r n)"), a1[0:TOK, 0:NR * P]).then_inc(v_ready.sem, 1)
                elif s in (2, 3):
                    b = s - 2
                    act.wait_ge(logit_done.sem, logit_done.after(g, b + 1))
                    act.activation(attn[:, b, TOK:TO], a0[0:TOK, TOK:TO], ACT.Relu).then_inc(off_ready.sem, 1)
                    act.wait_ge(diag_ready.sem, diag_ready.after(g, NR * b + 1))
                    act.activation(attn[:, b, TO + TOK:TO + 2 * TOK], a1[0:TOK, TOK:2 * TOK],
                                   ACT.Relu).then_inc(off_ready.sem, 1)
                elif s == 5:
                    square("A", g)
                elif s == 8:
                    for b in range(PAIR):
                        act.wait_ge(split_turned.sem, split_turned.after(g, b + 1))
                        act.copy(xs[g % 2][:, b, 0:TO], (a0, a1)[b][:, 0:TO]).then_inc(xs_ready.sem, 1)
                elif s == 10:
                    act.wait_ge(diff_ready.sem, diff_ready.after(g, 1))
                    act.activation(top[:, 3, :], top[:, 2, :], ACT.Exp).then_inc(exp_ready.sem, 1)
                elif s == 12:
                    act.wait_ge(gates_turned.sem, gates_turned.after(g, 1))
                    if g:
                        act.wait_ge(gates_out.sem, gates_out.after(g - 1, NR))
                    act.copy(gates_t[:], a1[0:NJ * E, 0:TOK]).then_inc(gates_t_ready.sem, 1)

            def stage_f(g, s):
                if s == 0:
                    act.wait_ge(y_added.sem, y_added.after(g, E))
                    act.copy(y_t[:], y[g % 2][:, 0:TO]).then_inc(yt_ready.sem, 1)
                elif s == 1:
                    square("F", g)

            def expert(g, e):
                act.wait_ge(z_done.sem, z_done.after(g, PAIR * e + 2))
                if g or e >= 2:
                    act.wait_ge(hid1_ready.sem, hid1_ready.after(g, e - 1))
                act.activation(rel[:, e % 2], z[1][:, 0:TO], ACT.Relu, bias=b1_col[:, e:e + 1]).then_inc(rel_ready.sem, 1)

            act.wait_ge(ld_tok, 16 * 18)
            act.wait_ge(ld_w1, 32)
            act.copy(w1_hi[:], w1_raw[:]).then_inc(w1_ready, 1)
            act.wait_ge(const_dve, 6)
            walk({"T": stage_t, "A": stage_a, "F": stage_f, "in": expert})

        @block.gpsimd
        def _(pool):
            made = [0]

            def chain(ins):
                made[0] += 1
                ins.then_inc(pool_chain, 1)
                pool.wait_ge(pool_chain, made[0])

            nc.gpsimd.memset(w_tok[:], 0.0).then_inc(zeroed, 1)
            nc.gpsimd.memset(filt_row[:], 0.0).then_inc(zeroed, 1)
            nc.gpsimd.memset(b2_diag[:], 0.0).then_inc(zeroed, 1)
            nc.gpsimd.memset(w_qk[:], 0.0).then_inc(zeroed, 1)
            nc.gpsimd.memset(w_vo[:], 0.0).then_inc(zeroed, 1)
            nc.gpsimd.memset(w2b1[:], 0.0).then_inc(zeroed, 1)
            pool.wait_ge(zeroed, 2)
            pool.dma_start(filt_row[0:1, MID:MID + TAPS], filt.unsqueeze(0)).then_inc(ld_filt, 16)
            chain(nc.gpsimd.memset(ident[:], 0.0))
            nc.gpsimd.affine_select(out=ident[:], in_=ident[:], compare_op=ALU.not_equal, fill=1.0, base=0,
                                    pattern=[[-1, P]], channel_multiplier=1).then_inc(const_pool, 1)
            pool.wait_ge(ld_filt, 16)
            pool.dma_start(filt_pad[:], filt_row[:]).then_inc(ld_filt, 16)
            chain(nc.gpsimd.memset(causal_cap[:], BIG))
            nc.gpsimd.affine_select(out=causal_cap[:], in_=causal_cap[:], compare_op=ALU.is_ge, fill=0.0, base=0,
                                    pattern=[[1, TOK]], channel_multiplier=-1).then_inc(const_pool, 1)
            nc.gpsimd.iota(row_pos[:], pattern=[[TOK, NR]], base=0, channel_multiplier=1).then_inc(const_pool, 1)
            nc.gpsimd.iota(prio_i[:], pattern=[[-1, E]], base=E, channel_multiplier=0).then_inc(const_pool, 1)
            nc.gpsimd.memset(minus_half[:], -0.5).then_inc(const_pool, 1)
            for buf in xs:
                nc.gpsimd.memset(buf[:, :, TO:W].bitcast(F32), 0.0).then_inc(const_pool, 1)
            pool.wait_ge(ld_filt, 32)
            shifts = bass.AP(filt_pad, 0, [[1, TOK], [1, BANDW]])
            pool.dma_start(band[:, 0:BANDW], shifts).then_inc(ld_band, 16)
            pool.wait_ge(const_pool, 7)

            def inverse_root(k, g):
                pool.wait_ge(ln_var[k].sem, ln_var[k].after(g, 1))
                nc.gpsimd.tensor_tensor(stat[k][:, 2, :], stat[k][:, 1, :], minus_half[:],
                                        ALU.pow).then_inc(ln_rstd[k].sem, 1)

            def stage_t(g, s):
                if s == 7:
                    inverse_root("T", g)

            def stage_a(g, s):
                if s == 6:
                    inverse_root("A", g)

            def stage_f(g, s):
                if s == 2:
                    inverse_root("F", g)
                elif s == 4:
                    pool.wait_ge(ln_done["F"].sem, ln_done["F"].after(g, 1))
                    nc.gpsimd.tensor_tensor(yn[:], yn[:], gamma_b[:].broadcast_to([TOK, NJ, D]),
                                            ALU.mult).then_inc(y_scaled.sem, 1)
                    pool.wait_ge(y_scaled.sem, y_scaled.after(g, 1))
                    nc.gpsimd.tensor_tensor(yn[:], yn[:], h2[g % 3][:], ALU.add).then_inc(y_scaled.sem, 1)
                    pool.wait_ge(y_scaled.sem, y_scaled.after(g, 2))
                    if g:
                        pool.wait_ge(stored.sem, stored.after(g - 1, PAIR))
                    nc.gpsimd.tensor_tensor(y_out[:], yn[:], beta_b[:].broadcast_to([TOK, NJ, D]),
                                            ALU.add).then_inc(y_out_ready.sem, 1)

            def expert(g, e):
                pool.wait_ge(rel_ready.sem, rel_ready.after(g, e + 1))
                if e % GE == 0:
                    k = e // GE
                    pool.wait_ge(gate_all_ready[k].sem, gate_all_ready[k].after(g, 1))
                if g or e >= HID:
                    pool.wait_ge(y_added.sem, y_added.after(g, e - HID + 1))
                nc.gpsimd.tensor_tensor(hid[:, (E * g + e) % HID, 1], rel[:, e % 2], gate_all[:, e, 1],
                                        ALU.mult).then_inc(hid1_ready.sem, 1)

            walk({"T": stage_t, "A": stage_a, "F": stage_f, "in": expert})

        @block.vector
        def _(dve):
            class Chain:

                def __init__(self, sig):
                    self.sig, self.k, self.g = sig, 0, None

                def at(self, g):
                    if g != self.g:
                        assert self.k in (0, self.sig.per), (self.sig.sem, self.k)
                        self.g, self.k = g, 0
                    return self

                def __call__(self, ins):
                    self.k += 1
                    ins.then_inc(self.sig.sem, 1)
                    dve.wait_ge(self.sig.sem, self.sig.after(self.g, self.k))

            chains = {"T": Chain(t_chain), "A": Chain(a_chain), "F": Chain(f_chain)}

            def wide(ap, n=D):
                return ap.unsqueeze(2).broadcast_to([TOK, NJ, n])

            def center(k, g, src):
                link, st = chains[k].at(g), stat[k]
                link(nc.vector.tensor_reduce(st[:, 0, :], src[:], AX.X, ALU.add))
                nc.vector.scalar_tensor_tensor(out=cent[k][:], in0=wide(st[:, 0, :]), scalar=1.0 / D, in1=src[:],
                                               op0=ALU.mult, op1=ALU.subtract, reverse1=True)\
                    .then_inc(ln_cent[k].sem, 1)

            def variance(k, g):
                link, st = chains[k].at(g), stat[k]
                dve.wait_ge(ln_sq[k].sem, ln_sq[k].after(g, 1))
                link(nc.vector.tensor_reduce(st[:, 0, :], csq[k][:], AX.X, ALU.add))
                nc.vector.tensor_scalar(st[:, 1, :], st[:, 0, :], 1.0 / D, EPS, ALU.mult,
                                        ALU.add).then_inc(ln_var[k].sem, 1)

            def normalise(k, g, dst):
                dve.wait_ge(ln_rstd[k].sem, ln_rstd[k].after(g, 1))
                nc.vector.tensor_tensor(dst[:], cent[k][:], wide(stat[k][:, 2, :]), ALU.mult).then_inc(ln_done[k].sem, 1)

            dve.wait_ge(ld_tok, 16 * 18)
            nc.vector.scalar_tensor_tensor(out=core_abs[:], in0=core_col[:], scalar=-1.0, in1=core_col[:],
                                           op0=ALU.mult, op1=ALU.max).then_inc(const_dve, 1)
            dve.wait_ge(const_dve, 1)
            nc.vector.tensor_scalar(w_tok[:, 2, :], w_tok[:, 2, :], core_abs[:, 0:1], None,
                                    ALU.mult).then_inc(const_dve, 1)
            dve.wait_ge(ld_band, 16)
            for k in range(4):
                last = nc.vector.tensor_copy(conv_w[:, k, :], conv_block(k))
            last.then_inc(const_dve, 1)
            dve.wait_ge(set_pe, 1)
            nc.vector.tensor_copy(wo_t[:], a0[0:D, 0:D]).then_inc(const_dve, 1)
            nc.vector.tensor_copy(b1_col[:], a0[:, 128:128 + E]).then_inc(const_dve, 1)
            nc.vector.tensor_scalar(b1_neg[:], a0[:, 128:128 + E], -1.0, None, ALU.mult).then_inc(const_dve, 1)
            dve.wait_ge(zeroed, 6)
            dve.wait_ge(set_pe, 2)
            for b in range(PAIR):
                r = slice(b * D, (b + 1) * D)
                nc.vector.tensor_copy(w_qk[r, r], a1[r, 0:D])
                last = nc.vector.tensor_copy(w_vo[r, r], a1[r, 128:128 + D])
            last.then_inc(const_dve, 1)
            dve.wait_ge(set_pe, 3)
            nc.vector.tensor_copy(w2b1[:, :, 0, :], a1[0:D, 256:256 + E].unsqueeze(1).broadcast_to([D, NR, E]))\
                .then_inc(const_dve, 1)
            dve.wait_ge(set_pe, 4)
            dve.wait_ge(ld_gate, 16 * 11)
            for r in range(NR):
                j, rows = PAIR * r, slice(PAIR * r * E, (PAIR * r + 1) * E)
                last = nc.vector.tensor_tensor(b2_diag[rows, j, :], b2_diag[rows, j, :], a0[rows, 256:256 + D], ALU.add)
            last.then_inc(const_dve, 1)
            dve.wait_ge(const_pool, 7)
            nc.vector.tensor_copy(row_cnt[:], row_pos[:]).then_inc(const_dve, 1)
            nc.vector.tensor_copy(prio[:, 0, :], prio_i[:]).then_inc(const_dve, 1)
            dve.wait_ge(const_dve, 11)
            nc.vector.tensor_scalar(row_cnt[:], row_cnt[:], 1.0, None, ALU.max).then_inc(const_dve, 1)
            nc.vector.tensor_copy(gate_s[:, 0, :], gate_raw[:]).then_inc(const_dve, 1)
            dve.wait_ge(const_dve, 13)
            nc.vector.reciprocal(row_inv[:], row_cnt[:]).then_inc(const_dve, 1)
            nc.vector.tensor_tensor(gate_s[:, 1, :], gate_raw[:], gate_s[:, 0, :].bitcast(F32),
                                    ALU.subtract).then_inc(const_dve, 1)
            dve.wait_ge(const_dve, 15)
            dve.wait_ge(w1_ready, 1)
            nc.vector.tensor_tensor(w1_lo[:], w1_raw[:], w1_hi[:].bitcast(F32), ALU.subtract).then_inc(w1_ready, 1)

            def stage_t(g, s):
                p = g % 2
                if s == 4:
                    flat = bias_last[:].rearrange("p b d -> p (b d)").unsqueeze(1).broadcast_to([TOK, NR, P])
                    for h in range(2):
                        dve.wait_ge(mm4.sem, mm4.after(g, h + 1))
                        sums = banks_of(g)[h][0:TOK, 0:NR * P].rearrange("p (c n) -> p c n", c=NR)
                        nc.vector.tensor_tensor(pre4[p][:, NR * h:NR * (h + 1), :], sums, flat,
                                                ALU.add).then_inc(biased4.sem, 1)
                elif s == 6:
                    dve.wait_ge(hres_ready.sem, hres_ready.after(g, 1))
                    center("T", g, hres[p])
                elif s == 7:
                    variance("T", g)
                elif s == 8:
                    normalise("T", g, xn1[p])

            def pick_a(link, values, best):
                link(nc.vector.tensor_reduce(best, values, AX.X, ALU.max))
                link(nc.vector.tensor_tensor(work[:, 0], values, wide(best, E), ALU.is_equal))

            def pick_b(link, chosen):
                link(nc.vector.tensor_tensor(work[:, 1], work[:, 0], prio[:].broadcast_to([TOK, NJ, E]), ALU.mult))
                link(nc.vector.tensor_reduce(top[:, 4, :], work[:, 1], AX.X, ALU.max))
                link(nc.vector.tensor_tensor(chosen, work[:, 1], wide(top[:, 4, :], E), ALU.is_equal))

            def stage_a(g, s):
                link = chains["A"].at(g)
                first, second = top[:, 0, :], top[:, 1, :]
                if s in (2, 3):
                    b = s - 2
                    dve.wait_ge(logit_done.sem, logit_done.after(g, b + 1))
                    for o, src in ((TO, a1[0:TOK, 0:TOK]), (0, a0[0:TOK, 0:TOK]),
                                   (TO + 2 * TOK, a0[0:TOK, TO:TO + TOK])):
                        if o == 0:
                            dve.wait_ge(off_ready.sem, off_ready.after(g, 2 * b + 1))
                        nc.vector.scalar_tensor_tensor(out=attn[:, b, o:o + TOK], in0=src, scalar=0.0,
                                                       in1=causal_cap[:], op0=ALU.max,
                                                       op1=ALU.min).then_inc(diag_ready.sem, 1)
                elif s == 4:
                    dve.wait_ge(ctx_done.sem, ctx_done.after(g, 1))
                    for r in range(NR):
                        js = slice(PAIR * r, PAIR * (r + 1))
                        ins = nc.vector.scalar_tensor_tensor(
                            out=h2[g % 3][:, js, :].rearrange("p j d -> p (j d)"), in0=a0[0:TOK, r * P:(r + 1) * P],
                            scalar=row_inv[:, r:r + 1], in1=hres[g % 2][:, js, :].rearrange("p j d -> p (j d)"),
                            op0=ALU.mult, op1=ALU.add)
                    link(ins)
                elif s == 5:
                    center("A", g, h2[g % 3])
                elif s == 6:
                    variance("A", g)
                elif s == 7:
                    normalise("A", g, xn2)
                    dve.wait_ge(ln_done["A"].sem, ln_done["A"].after(g, 1))
                    link(nc.vector.tensor_copy(split[:, :, 0, :], xn2[:]))
                    nc.vector.tensor_tensor(split[:, :, 1, :], xn2[:], split[:, :, 0, :].bitcast(F32),
                                            ALU.subtract).then_inc(split_ready.sem, 1)
                elif s == 9:
                    dve.wait_ge(gate_done.sem, gate_done.after(g, 1))
                    sums = a0[0:TOK, 0:NJ * 2 * E].rearrange("p (j s e) -> p j s e", s=2, e=E)
                    link(nc.vector.tensor_tensor(work[:, 3], sums[:, :, 1, :], gate_bb[:].broadcast_to([TOK, NJ, E]), ALU.add))
                    link(nc.vector.tensor_tensor(logits[:], sums[:, :, 0, :], work[:, 3], ALU.add))
                    pick_a(link, logits[:], first)
                    pick_b(link, pick1[:])
                elif s == 10:
                    link(nc.vector.scalar_tensor_tensor(out=work[:, 2], in0=pick1[:], scalar=-BIG, in1=logits[:],
                                                        op0=ALU.mult, op1=ALU.add))
                    pick_a(link, work[:, 2], second)
                    nc.vector.tensor_tensor(top[:, 2, :], second, first, ALU.subtract).then_inc(diff_ready.sem, 1)
                    pick_b(link, pick2[:])
                elif s == 11:
                    dve.wait_ge(exp_ready.sem, exp_ready.after(g, 1))
                    link(nc.vector.tensor_scalar(top[:, 5, :], top[:, 3, :], 1.0, None, ALU.add))
                    link(nc.vector.reciprocal(top[:, 6, :], top[:, 5, :]))
                    link(nc.vector.tensor_tensor(top[:, 7, :], top[:, 3, :], top[:, 6, :], ALU.mult))
                    link(nc.vector.tensor_tensor(work[:, 0], pick1[:], wide(top[:, 6, :], E), ALU.mult))
                    link(nc.vector.tensor_tensor(work[:, 1], pick2[:], wide(top[:, 7, :], E), ALU.mult))
                    nc.vector.tensor_tensor(gates[:], work[:, 0], work[:, 1], ALU.add).then_inc(gates_made.sem, 1)
                elif s == 13:
                    dve.wait_ge(b2_done.sem, b2_done.after(g, 1))
                    nc.vector.tensor_tensor(y_base[g % 2][:].rearrange("p j d -> p (j d)"), a0[0:TOK, 0:NJ * D],
                                            xn2[:].rearrange("p j d -> p (j d)"), ALU.add).then_inc(y_base_ready.sem, 1)

            def stage_f(g, s):
                link = chains["F"].at(g)
                if s == 1:
                    dve.wait_ge(y_turned.sem, y_turned.after(g, 1))
                    link(nc.vector.tensor_tensor(y_tok[:].rearrange("p j d -> p (j d)"), y[g % 2][0:TOK, 0:NJ * D],
                                                 y_base[g % 2][:].rearrange("p j d -> p (j d)"), ALU.add))
                    center("F", g, y_tok)
                elif s == 2:
                    variance("F", g)
                elif s == 3:
                    normalise("F", g, yn)

            def expert(g, e):
                dve.wait_ge(z_done.sem, z_done.after(g, PAIR * e + 1))
                if e % GE == 0:
                    k = e // GE
                    dve.wait_ge(gate_all_ready[k].sem, gate_all_ready[k].after(g, 1))
                if g or e >= HID:
                    dve.wait_ge(y_added.sem, y_added.after(g, e - HID + 1))
                nc.vector.scalar_tensor_tensor(out=hid[:, (E * g + e) % HID, 0], in0=z[0][:, 0:TO],
                                               scalar=b1_neg[:, e:e + 1], in1=gate_all[:, e, 0], op0=ALU.max,
                                               op1=ALU.mult).then_inc(hid0_ready.sem, 1)

            walk({"T": stage_t, "A": stage_a, "F": stage_f, "in": expert})

        @block.tensor
        def _(pe):
            mm = nc.tensor.matmul

            pe.wait_ge(const_pool, 1)
            pe.wait_ge(ld_attn, 16 * 7)
            nc.tensor.transpose(a0[0:D, 0:D], wo_s[:], ident[0:D, 0:D])
            nc.tensor.transpose(a0[:, 128:128 + E], b1_s[:], ident[0:E, 0:E]).then_inc(set_pe, 1)
            pe.wait_ge(const_dve, 4)
            mm(a1[:, 0:D], wq2[:].rearrange("p b d -> p (b d)"), wk_s[:], start=True, stop=True)
            mm(a1[:, 128:128 + D], wv2[:].rearrange("p b d -> p (b d)"), wo_t[:],
               start=True, stop=True).then_inc(set_pe, 1)
            pe.wait_ge(const_dve, 7)
            pe.wait_ge(ld_w2, 16)
            for e in range(E):
                last = mm(a1[0:D, 256 + e:257 + e], w2_s[:, e, :], b1_col[:, e:e + 1], start=True, stop=True)
            last.then_inc(set_pe, 1)
            pe.wait_ge(const_dve, 8)
            mm(a0[0:NJ * E, 256:256 + D], w2b1[:].rearrange("d r b e -> d (r b e)"), ident[0:D, 0:D],
               start=True, stop=True).then_inc(set_pe, 1)
            pe.wait_ge(ld_tok, 16 * 18)
            pe.wait_ge(const_dve, 15)

            def stage_t(g, s):
                p, banks = g % 2, banks_of(g)
                if s == 0:
                    pe.wait_ge(x_in_ready[p], 16 * PAIR * (g // 2 + 1))
                    if g >= 2:
                        g0 = 0 if g == 2 else 2
                        pe.wait_ge(hres_ready.sem, hres_ready.after(g0, 1))
                    for c in range(NT):
                        ins = nc.tensor.transpose(banks[c // NR][:, c % NR * TOK:(c % NR + 1) * TOK],
                                                  x_in[p][:, c].rearrange("p b d -> p (b d)"), ident[0:TOK, 0:TOK])
                        if c % NR == NR - 1:
                            ins.then_inc(x_turned.sem, 1)
                elif s in (1, 2, 3):
                    src, ready, said = {1: (x_t, xt_ready, mm1), 2: (act1, tanh1, mm2), 3: (sq, squared, mm3)}[s]
                    for h in range(2):
                        pe.wait_ge(ready.sem, ready.after(g, h + 1))
                        mm(banks[h][:, 0:HT], w_tok[:, s - 1, :], src[p][:, halves[h]],
                           start=True, stop=True).then_inc(said.sem, 1)
                elif s == 4:
                    for c in range(NT):
                        if c % NR == 0:
                            pe.wait_ge(tanh3.sem, tanh3.after(g, c // NR + 1))
                        ins = mm(banks[c // NR][0:TOK, c % NR * P:(c % NR + 1) * P],
                                 act3[p][:, c * TOK:(c + 1) * TOK], w_tok[:, 3, :], start=True, stop=True)
                        if c % NR == NR - 1:
                            ins.then_inc(mm4.sem, 1)
                elif s == 5:
                    pe.wait_ge(tanh4.sem, tanh4.after(g, 2))
                    for r in range(NR):
                        cs = [c for c in range(2 * r - 1, 2 * r + 3) if 0 <= c < NT]
                        for c in cs:
                            ins = mm(banks[0][0:TOK, r * P:(r + 1) * P], conv_w[:, c - 2 * r + 1, :],
                                     act4[p][:, c, :], start=c == cs[0], stop=c == cs[-1])
                    ins.then_inc(conv_done.sem, 1)

            def stage_a(g, s):
                if s == 0:
                    pe.wait_ge(ln_done["T"].sem, ln_done["T"].after(g, 1))
                    if g:
                        pe.wait_ge(y_base_ready.sem, y_base_ready.after(g - 1, 1))
                    for r in range(NR):
                        ins = nc.tensor.transpose(a0[:, r * TOK:(r + 1) * TOK],
                                                  xn1[g % 2][:, PAIR * r:PAIR * (r + 1)].rearrange("p b d -> p (b d)"),
                                                  ident[0:TOK, 0:TOK])
                    ins.then_inc(xn1_turned.sem, 1)
                elif s == 1:
                    pe.wait_ge(xn1t_ready.sem, xn1t_ready.after(g, 1))
                    mm(a0[:, 0:TO], w_qk[:], xn1_t[:], start=True, stop=True).then_inc(qv_done.sem, 1)
                    if g:
                        pe.wait_ge(gates_t_ready.sem, gates_t_ready.after(g - 1, 1))
                    for r in range(NR):
                        ins = mm(a1[0:TOK, r * P:(r + 1) * P], xn1_t[:, r * TOK:(r + 1) * TOK], w_vo[:],
                                 start=True, stop=True)
                    ins.then_inc(qv_done.sem, 1)
                elif s in (2, 3):
                    b = s - 2
                    if b == 0:
                        pe.wait_ge(qt_ready.sem, qt_ready.after(g, 1))
                        pe.wait_ge(v_ready.sem, v_ready.after(g, 1))
                    else:
                        pe.wait_ge(off_ready.sem, off_ready.after(g, 2))
                        pe.wait_ge(diag_ready.sem, diag_ready.after(g, NR))
                    f = slice(b * D, (b + 1) * D)
                    for m, dst in ((0, a0[0:TOK, 0:TO]), (1, a1[0:TOK, 0:2 * TOK]), (2, a0[0:TOK, TO:TO + TOK])):
                        ins = mm(dst, xn1_t[f, m * TOK:(m + 1) * TOK], q_t[f, m * TOK:TO], start=True, stop=True)
                    ins.then_inc(logit_done.sem, 1)
                elif s == 4:
                    pe.wait_ge(off_ready.sem, off_ready.after(g, 2 * PAIR))
                    pe.wait_ge(diag_ready.sem, diag_ready.after(g, NR * PAIR))
                    at = [0, TO, TO + 2 * TOK]
                    for r in range(NR):
                        for b in range(PAIR):
                            for m in range(r + 1):
                                ins = mm(a0[0:TOK, r * P + b * D:r * P + (b + 1) * D],
                                         attn[:, b, at[m] + (r - m) * TOK:at[m] + (r - m + 1) * TOK],
                                         v_s[:, m, b * D:(b + 1) * D], start=m == 0, stop=m == r)
                    ins.then_inc(ctx_done.sem, 1)
                elif s == 8:
                    pe.wait_ge(split_ready.sem, split_ready.after(g, 1))
                    for b in range(PAIR):
                        for r in range(NR):
                            ins = nc.tensor.transpose(
                                (a0, a1)[b][:, r * TOK:(r + 1) * TOK],
                                split[:, PAIR * r + b].rearrange("p s d -> p (s d)").bitcast(F32),
                                ident[0:TOK, 0:TOK])
                        ins.then_inc(split_turned.sem, 1)
                elif s == 9:
                    pe.wait_ge(xs_ready.sem, xs_ready.after(g, PAIR))
                    for j in range(NJ):
                        r, b = j // PAIR, j % PAIR
                        ins = mm(a0[0:TOK, j * 2 * E:(j + 1) * 2 * E], xs[g % 2][:, b, r * TOK:(r + 1) * TOK],
                                 gate_s[:].rearrange("p s e -> p (s e)"), start=True, stop=True)
                    ins.then_inc(gate_done.sem, 1)
                elif s == 12:
                    pe.wait_ge(gates_made.sem, gates_made.after(g, 1))
                    nc.tensor.transpose(a1[0:NJ * E, 0:TOK], gates[:].rearrange("p j e -> p (j e)"),
                                        ident[0:TOK, 0:TOK]).then_inc(gates_turned.sem, 1)
                elif s == 13:
                    pe.wait_ge(gates_t_ready.sem, gates_t_ready.after(g, 1))
                    mm(a0[0:TOK, 0:NJ * D], gates_t[:], b2_diag[:].rearrange("p j d -> p (j d)"),
                       start=True, stop=True).then_inc(b2_done.sem, 1)

            def stage_f(g, s):
                if s == 0:
                    pe.wait_ge(yt_ready.sem, yt_ready.after(g, 1))
                    for r in range(NR):
                        ins = nc.tensor.transpose(y[g % 2][0:TOK, r * P:(r + 1) * P],
                                                  y_t[:, r * TOK:(r + 1) * TOK], ident[:])
                    ins.then_inc(y_turned.sem, 1)

            def expert_in(g, e):
                if e == 0:
                    pe.wait_ge(xs_ready.sem, xs_ready.after(g, PAIR))
                    if g == 0:
                        pe.wait_ge(w1_ready, 2)
                        pe.wait_ge(hres_ready.sem, hres_ready.after(1, 1))
                for b in range(PAIR):
                    if g or e:
                        read = (hid0_ready, rel_ready)[b]
                        pe.wait_ge(read.sem, read.after(g, e))
                    mm(z[b][:, 0:W], w1_hi[:, e, :], xs[g % 2][:, b, :], start=True, stop=False)
                    mm(z[b][:, 0:W], w1_lo[:, e, :], xs[g % 2][:, b, :], start=False, stop=True).then_inc(z_done.sem, 1)

            def expert_out(g, e):
                pe.wait_ge(hid0_ready.sem, hid0_ready.after(g, e + 1))
                pe.wait_ge(hid1_ready.sem, hid1_ready.after(g, e + 1))
                if g >= 2 and e == 0:
                    pe.wait_ge(ln_cent["F"].sem, ln_cent["F"].after(g - 2, 1))
                for b in range(PAIR):
                    ins = mm(y[g % 2][b * D:(b + 1) * D, 0:TO], w2_s[:, e, :], hid[:, (E * g + e) % HID, b],
                             start=e == 0, stop=e == E - 1)
                ins.then_inc(y_added.sem, 1)

            walk({"T": stage_t, "A": stage_a, "F": stage_f, "in": expert_in, "out": expert_out})


_INS = ["x", "L0_tok_W_in", "L0_tok_b_in", "L0_tok_W_out", "L0_tok_b_out", "L0_tok_core_diag", "L0_tok_conv_filter",
        "L0_attn_Wq", "L0_attn_Wk", "L0_attn_Wv", "L0_attn_Wo", "L0_ffn_gate_w", "L0_ffn_gate_b", "L0_ffn_w1",
        "L0_ffn_b1", "L0_ffn_w2", "L0_ffn_b2", "L0_ffn_gamma", "L0_ffn_beta"]
_OUT = ((8, 375, 64), "float32")


def kernel(**inputs):
    import numpy as _np
    import concourse.bacc as _bacc
    from concourse import mybir as _mybir
    from concourse.bass_utils import run_bass_kernel_spmd as _run

    nc = _bacc.Bacc("TRN2", target_bir_lowering=False, num_devices=1)
    arrays, args = {}, []
    for name in _INS:
        a = _np.ascontiguousarray(inputs[name])
        arrays[f"in_{name}_dram"] = a
        args.append(nc.dram_tensor(f"in_{name}_dram", a.shape, _mybir.dt.from_np(a.dtype), kind="ExternalInput").ap())
    args.append(nc.dram_tensor("out_dram", _OUT[0], _mybir.dt.from_np(_np.dtype(_OUT[1])), kind="ExternalOutput").ap())
    audio_tower(nc, *args)
    r = _run(nc, [arrays], core_ids=[0])
    return r.results[0]["out_dram"]
```

```python
from contextlib import ExitStack

import concourse.bass as bass
from concourse import mybir

F32 = mybir.dt.float32
F32R = mybir.dt.float32r
I32 = mybir.dt.int32
ALU = mybir.AluOpType
ACT = mybir.ActivationFunctionType
AX = mybir.AxisListType

P = 128
TOK = 125
PAIR = 2
GATE_LAG = 3
OUT_LAG = 5
REL = 5
HID = 3
EARLY = 4
CHUNKS = [0, 1, 2, 4, 6, 8, 10, 12, 14]
ROW = 768
BIG = 3.4028234663852886e38
EPS = 1e-5


class Signal:

    def __init__(self, sem, per, unit=1):
        self.sem, self.per, self.unit = sem, per, unit

    def after(self, g, k):
        return (self.per * g + k) * self.unit


def audio_tower(nc, x, w_in, b_in, w_out, b_out, core, filt, wq, wk, wv, wo,
                gate_w, gate_b, w1, b1, w2, b2, gamma, beta, out):
    B, T, D = x.shape
    TO = out.shape[1]
    E, _, F = w1.shape
    NG = B // PAIR
    NT = T // TOK
    NR = TO // TOK
    NJ = NR * PAIR
    HT = T // 2
    W = TO + 1
    TAPS = filt.shape[0]
    assert D * PAIR == P and F == P and T == 2 * TO and HT == NR * TOK

    ctx = ExitStack()
    with ctx:
        def sb(name, shape, dt=F32):
            return ctx.enter_context(nc.sbuf_tensor(name, shape, dt))

        def bank(name):
            return ctx.enter_context(nc.psum_tensor(name, [P, 512], F32))

        def sem(name):
            return ctx.enter_context(nc.semaphore(name))

        def signal(name, per=1, unit=1):
            return Signal(sem(name), per, unit)

        ident = sb("ident", [P, P])
        w_tok = sb("w_tok", [P, 4, P])
        centring = sb("centring", [P, P])
        vec_rows = sb("vec_rows", [5, PAIR, D])
        vec_cols = sb("vec_cols", [P, 5])
        bias_last = sb("bias_last", [TOK, PAIR, D])
        core_abs = sb("core_abs", [P, 1])
        filt_row = sb("filt_row", [1, ROW])
        filt_pad = nc.dram_tensor("filt_pad", [1, ROW], F32)
        band = sb("band", [TOK, 640])
        conv_w = sb("conv_w", [TOK, 4, TOK])
        wq2 = sb("wq2", [D, PAIR, D])
        wk_s = sb("wk_s", [D, D])
        wv2 = sb("wv2", [D, PAIR, D])
        wo_s = sb("wo_s", [D, D])
        wo_t = sb("wo_t", [D, D])
        w_qk = sb("w_qk", [P, P])
        w_vo = sb("w_vo", [P, P])
        minus_half = sb("minus_half", [TOK, NJ])
        causal_cap = sb("causal_cap", [TOK, TOK])
        row_pos = sb("row_pos", [TOK, NR], I32)
        row_cnt = sb("row_cnt", [TOK, NR])
        row_inv = sb("row_inv", [TOK, NR])
        prio_i = sb("prio_i", [TOK, E], I32)
        prio = sb("prio", [TOK, 1, E])
        gate_raw = sb("gate_raw", [P, E])
        gate_s = sb("gate_s", [P, 2, E], F32R)
        gate_bb = sb("gate_bb", [TOK, 1, E])
        w1_raw = sb("w1_raw", [P, E, F])
        w1_hi = sb("w1_hi", [P, E, F], F32R)
        w1_lo = sb("w1_lo", [P, E, F], F32R)
        w2_s = sb("w2_s", [F, E, D])
        b1_s = sb("b1_s", [E, F])
        b1_col = sb("b1_col", [F, E])
        b2_s = sb("b2_s", [E, D])
        rep6 = sb("rep6", [E, NJ, E])
        own_tile = sb("own_tile", [NJ * E, NJ])
        b2_mean = sb("b2_mean", [NJ * E, 1])
        b2_cent = sb("b2_cent", [NJ * E, D])
        b2_diag = sb("b2_diag", [NJ * E, NJ, D])
        gamma_b = sb("gamma_b", [TOK, 1, D])
        beta_b = sb("beta_b", [TOK, 1, D])

        x_in = [sb(f"x_in{i}", [TOK, NT, PAIR, D]) for i in range(2)]
        buf_a = [sb(f"buf_a{i}", [P, NT * P]) for i in range(NG)]
        buf_b = [sb(f"buf_b{i}", [P, NT * P]) for i in range(NG)]
        hres = [sb(f"hres{i}", [TOK, NJ, D]) for i in range(NG)]
        xn1 = [sb(f"xn1_{i}", [TOK, NJ, D]) for i in range(NG)]

        def by_tile(buf):
            return buf[0:TOK, :].rearrange("p (c n) -> p c n", c=NT)

        xn1_t = sb("xn1_t", [P, TO])
        q_t = sb("q_t", [P, TO])
        v_s = sb("v_s", [TOK, NR, P])
        attn = sb("attn", [TOK, PAIR, NJ * TOK])
        h2 = [sb(f"h2_{i}", [TOK, NJ, D]) for i in range(3)]
        xn2 = sb("xn2", [TOK, NJ, D])
        split = sb("split", [TOK, NJ, 2, D], F32R)
        xs = [sb(f"xs{i}", [P, PAIR, W], F32R) for i in range(2)]
        logits = sb("logits", [TOK, NJ, E])
        top = sb("top", [TOK, 8, NJ])
        pick1 = sb("pick1", [TOK, NJ, E])
        pick2 = sb("pick2", [TOK, NJ, E])
        work = sb("work", [TOK, 4, NJ, E])
        gates = sb("gates", [TOK, NJ, E])
        gates_t = sb("gates_t", [NJ * E, TOK])
        y_base = [sb(f"y_base{i}", [TOK, NJ, D]) for i in range(2)]
        gates_dram = nc.dram_tensor("gates_dram", [NG, E, PAIR, TO], F32)
        gate_all = sb("gate_all", [P, E, PAIR, TO])
        hid = sb("hid", [F, HID, PAIR, TO])
        rel = sb("rel", [F, REL, PAIR, TO])
        y_t = sb("y_t", [P, TO])
        scaled = sb("scaled", [TOK, NJ, D])
        yn = sb("yn", [TOK, NJ, D])
        h2_beta = sb("h2_beta", [TOK, NJ, D])
        y_out = sb("y_out", [TOK, NJ, D])
        cent = {k: sb(f"cent_{k}", [TOK, NJ, D]) for k in "TAF"}
        csq = {k: sb(f"csq_{k}", [TOK, NJ, D]) for k in "TAF"}
        stat = {k: sb(f"stat_{k}", [TOK, 3, NJ]) for k in "TAF"}

        z = [[bank("z00"), bank("z01")], [bank("z10"), bank("z11")]]
        y = [bank("y0"), bank("y1")]
        a0, a1 = bank("a0"), bank("a1")

        def banks_of(g):
            return (z[1], z[0], y, z[1])[g]

        ld_in = sem("ld_in")
        ld_out = sem("ld_out")
        ld_vec = sem("ld_vec")
        ld_bias = sem("ld_bias")
        vec_turned = sem("vec_turned")
        ld_turn = sem("ld_turn")
        ld_b2 = sem("ld_b2")
        ld_last = sem("ld_last")
        ld_filt = sem("ld_filt")
        ld_band = sem("ld_band")
        ld_attn = sem("ld_attn")
        ld_gate = sem("ld_gate")
        ld_gate_b = sem("ld_gate_b")
        ld_w1 = sem("ld_w1")
        ld_w2 = sem("ld_w2")
        zeroed = sem("zeroed")
        const_pool = sem("const_pool")
        pool_chain = sem("pool_chain")
        core_ready = sem("core_ready")
        turned = sem("turned")
        turned_ready = sem("turned_ready")
        prod_done = sem("prod_done")
        prod_ready = sem("prod_ready")
        centring_ready = sem("centring_ready")
        b2_rows = sem("b2_rows")
        b2_diag_ready = sem("b2_diag_ready")
        conv_w_ready = sem("conv_w_ready")
        small = sem("small")
        w1_ready = sem("w1_ready")
        x_in_ready = [sem(f"x_in_ready{i}") for i in range(NG)]
        x_turned = signal("x_turned", 2)
        xt_ready = signal("xt_ready", 2)
        mm1 = signal("mm1", 2)
        tanh1 = signal("tanh1", 2)
        mm2 = signal("mm2", 2)
        tanh2 = signal("tanh2", 2)
        squared = signal("squared", 2)
        mm3 = signal("mm3", 2)
        tanh3 = signal("tanh3", 2)
        mm4 = signal("mm4", 2)
        biased4 = signal("biased4", 2)
        tanh4 = signal("tanh4", 2)
        conv_done = signal("conv_done")
        hres_ready = signal("hres_ready")
        ln_cent = {k: signal(f"ln_cent_{k}") for k in "TAF"}
        ln_sq = {k: signal(f"ln_sq_{k}") for k in "TAF"}
        ln_var = {k: signal(f"ln_var_{k}") for k in "TAF"}
        ln_rstd = {k: signal(f"ln_rstd_{k}") for k in "TAF"}
        ln_done = {k: signal(f"ln_done_{k}") for k in "TAF"}
        xn1_turned = signal("xn1_turned")
        xn1t_ready = signal("xn1t_ready")
        qv_done = signal("qv_done", 2)
        qt_ready = signal("qt_ready")
        v_ready = signal("v_ready")
        logit_done = signal("logit_done", PAIR)
        off_ready = signal("off_ready", 2 * PAIR)
        diag_ready = signal("diag_ready", NR * PAIR)
        ctx_done = signal("ctx_done")
        split_ready = signal("split_ready")
        split_turned = signal("split_turned", PAIR)
        xs_ready = signal("xs_ready", PAIR)
        gate_done = signal("gate_done")
        diff_ready = signal("diff_ready")
        exp_ready = signal("exp_ready")
        gates_made = signal("gates_made")
        gates_turned = signal("gates_turned")
        gates_t_ready = signal("gates_t_ready")
        gates_out = signal("gates_out", NR, 16)
        gate_all_ready = [signal(f"gate_all_ready{k}", 1, 16) for k in range(len(CHUNKS))]
        b2_done = signal("b2_done")
        y_base_ready = signal("y_base_ready")
        z_done = signal("z_done", PAIR * E)
        hid0_ready = signal("hid0_ready", E)
        rel_ready = signal("rel_ready", PAIR * E)
        hid1_ready = signal("hid1_ready", E)
        y_added = signal("y_added", E)
        yt_ready = signal("yt_ready")
        y_turned = signal("y_turned")
        h2_beta_ready = signal("h2_beta_ready")
        y_out_ready = signal("y_out_ready")
        stored = signal("stored", PAIR, 16)
        t_chain = signal("t_chain", 2)
        a_chain = signal("a_chain", 22)
        f_chain = signal("f_chain", 3)

        beside = {0: [("A", 1, 3)], 1: [("T", 3, 6), ("A", 1, 4), ("T", 3, 7)], 2: [("A", 1, 5)],
                  3: [("A", 1, 6), ("T", 3, 8), ("F", -1, 0)], 4: [("A", 1, 7)], 5: [],
                  6: [("F", -1, 1), ("A", 1, 8), ("F", -1, 2)], 7: [("A", 1, 9)], 8: [], 9: [("A", 1, 10)],
                  10: [], 11: [("F", -1, 3), ("A", 1, 11)], 12: [("F", -1, 4)], 13: [("A", 1, 12)],
                  14: [("A", 1, 13), ("A", 2, 0), ("F", -1, 5)], 15: [("A", 2, 1), ("A", 2, 2)]}
        plan = [("T", 0, 0), ("T", 1, 0), ("S", 0, 0), ("T", 0, 1), ("S", 0, 8), ("S", 0, 5), ("T", 0, 2),
                ("T", 1, 1), ("T", 0, 3), ("T", 0, 4), ("S", 0, 1), ("T", 1, 2), ("S", 0, 2), ("S", 0, 3),
                ("T", 2, 0), ("T", 0, 5), ("T", 0, 6), ("T", 0, 7), ("S", 0, 4), ("T", 1, 3), ("T", 0, 8),
                ("T", 2, 1), ("T", 3, 0), ("T", 1, 4), ("S", 0, 6), ("A", 0, 0), ("T", 2, 2), ("T", 3, 1),
                ("A", 0, 1), ("T", 1, 5), ("A", 0, 2), ("T", 2, 3), ("A", 0, 3), ("S", 0, 7), ("T", 3, 2),
                ("A", 0, 4), ("T", 2, 4), ("A", 0, 5), ("T", 1, 6), ("T", 3, 3), ("A", 0, 6), ("T", 2, 5),
                ("T", 1, 7), ("A", 0, 7), ("T", 3, 4), ("T", 1, 8), ("A", 0, 8), ("A", 0, 9), ("T", 3, 5),
                ("in", 0, 0), ("A", 0, 10), ("A", 0, 11), ("in", 0, 1), ("in", 0, 2), ("A", 0, 12), ("T", 2, 6),
                ("A", 0, 13), ("T", 2, 7), ("A", 1, 0), ("A", 1, 1), ("in", 0, 3), ("T", 2, 8), ("A", 1, 2)]
        for n in range(NG * E + OUT_LAG):
            g, e = n // E, n % E
            if EARLY <= n < NG * E:
                plan.append(("in", g, e))
            if 0 <= n - GATE_LAG < NG * E:
                plan.append(("gate", (n - GATE_LAG) // E, (n - GATE_LAG) % E))
            if n < NG * E:
                plan += [(k, g + d, s) for k, d, s in beside[e] if 0 <= g + d < NG]
            if n >= OUT_LAG:
                plan.append(("out", (n - OUT_LAG) // E, (n - OUT_LAG) % E))
        plan += [("F", NG - 1, s) for s in range(6)]

        def walk(stages):
            for kind, g, s in plan:
                if kind in stages:
                    stages[kind](g, s)

        block = ctx.enter_context(nc.Block())
        halves = [slice(0, HT), slice(HT, T)]
        MID = 368
        BANDW = MID + TAPS // 2 + 2 * TOK + 1
        assert BANDW + TOK <= ROW and MID + TAPS // 2 >= 3 * TOK

        def conv_block(k):
            top_col = MID + TAPS // 2 + TOK * (k - 1)
            return band[:, top_col:top_col - 2 * TOK:-2]

        @block.sync
        def _(sp):
            def load_x(g):
                for b in range(PAIR):
                    src = x[PAIR * g + b].rearrange("(c p) d -> p c d", p=TOK)
                    sp.dma_start(x_in[g % 2][:, :, b, :], src).then_inc(x_in_ready[g], 16)

            def stage_a(g, s):
                if s == 12:
                    sp.wait_ge(gates_t_ready.sem, gates_t_ready.after(g, 1))
                    rows = gates_dram[g].rearrange("e b (r p) -> r b e p", r=NR)
                    for r in range(NR):
                        sp.dma_start(rows[r], gates_t[r * PAIR * E:(r + 1) * PAIR * E, :]).then_inc(gates_out.sem, 16)
                    sp.wait_ge(gates_out.sem, gates_out.after(g, NR))
                    for k, (e0, e1) in enumerate(zip(CHUNKS, CHUNKS[1:] + [E])):
                        if g:
                            sp.wait_ge(hid0_ready.sem, hid0_ready.after(g - 1, e1))
                            sp.wait_ge(hid1_ready.sem, hid1_ready.after(g - 1, e1))
                        src = gates_dram[g, e0:e1].rearrange("e b t -> (e b t)")
                        sp.dma_start(gate_all[:, e0:e1].rearrange("p e b t -> p (e b t)"),
                                     src.partition_broadcast(P)).then_inc(gate_all_ready[k].sem, 16)

            def stage_f(g, s):
                if s == 5:
                    sp.wait_ge(y_out_ready.sem, y_out_ready.after(g, 1))
                    view = y_out[:].rearrange("p (r b) d -> p r b d", b=PAIR)
                    for b in range(PAIR):
                        dst = out[PAIR * g + b].rearrange("(r p) d -> p r d", p=TOK)
                        sp.dma_start(dst, view[:, :, b, :]).then_inc(stored.sem, 16)

            load_x(0)
            load_x(1)
            sp.wait_ge(zeroed, 1)
            for b in range(PAIR):
                sp.dma_start(w_tok[b * D:(b + 1) * D, 2:4, b * D:(b + 1) * D],
                             w_out.rearrange("n d m -> d n m")).then_inc(ld_out, 16)
            sp.dma_start(wo_s[:], wo).then_inc(ld_turn, 16)
            sp.dma_start(b1_s[:], b1).then_inc(ld_turn, 16)
            sp.dma_start(wq2[:], wq.unsqueeze(1).broadcast_to([D, PAIR, D])).then_inc(ld_attn, 16)
            sp.dma_start(wv2[:], wv.unsqueeze(1).broadcast_to([D, PAIR, D])).then_inc(ld_attn, 16)
            sp.dma_start(wk_s[:], wk).then_inc(ld_attn, 16)
            sp.dma_start(w2_s[:], w2.rearrange("e f h -> f e h")).then_inc(ld_w2, 16)
            sp.wait_ge(x_turned.sem, x_turned.after(0, 2))
            load_x(2)
            for b in range(PAIR):
                sp.dma_start(w1_raw[b * D:(b + 1) * D, :, :], w1.rearrange("e h f -> h e f")).then_inc(ld_w1, 16)
            for b in range(PAIR):
                sp.dma_start(gate_raw[b * D:(b + 1) * D, :], gate_w).then_inc(ld_gate, 16)
            sp.wait_ge(x_turned.sem, x_turned.after(1, 2))
            load_x(3)
            walk({"A": stage_a, "F": stage_f})
            sp.wait_ge(stored.sem, stored.after(NG - 1, PAIR))

        @block.scalar
        def _(act):
            act.wait_ge(zeroed, 1)
            for b in range(PAIR):
                act.dma_start(w_tok[b * D:(b + 1) * D, 0:2, b * D:(b + 1) * D],
                              w_in.rearrange("n d m -> d n m")).then_inc(ld_in, 16)
            for rows, v in ((vec_rows[0:2], b_in), (vec_rows[2:4], b_out), (vec_rows[4:5], core.unsqueeze(0))):
                n = v.shape[0]
                act.dma_start(rows, v.unsqueeze(1).broadcast_to([n, PAIR, D])).then_inc(ld_vec, 16)
            act.dma_start(bias_last[:], b_out[0].unsqueeze(0).partition_broadcast(TOK).broadcast_to([TOK, PAIR, D]))\
                .then_inc(ld_bias, 16)

            def square(k, g):
                act.wait_ge(ln_cent[k].sem, ln_cent[k].after(g, 1))
                act.activation(csq[k][:], cent[k][:], ACT.Square).then_inc(ln_sq[k].sem, 1)

            def setup(_, s):
                if s == 0:
                    act.wait_ge(vec_turned, 1)
                    act.copy(vec_cols[:], a1[:, 0:5]).then_inc(vec_turned, 1)
                    act.wait_ge(vec_turned, 2)
                elif s == 7:
                    act.wait_ge(ld_w1, 32)
                    act.copy(w1_hi[:], w1_raw[:]).then_inc(w1_ready, 1)

            def stage_t(g, s):
                banks, buf_a_g, buf_b_g = banks_of(g), buf_a[g], buf_b[g]
                if s in (1, 2, 3):
                    done, dst, said = {1: (mm1, buf_b_g, tanh1), 2: (mm2, buf_a_g, tanh2), 3: (mm3, buf_a_g, tanh3)}[s]
                    bias = vec_cols[:, (0, 1, 3)[s - 1]:(0, 1, 3)[s - 1] + 1]
                    for h in range(2):
                        act.wait_ge(done.sem, done.after(g, h + 1))
                        act.activation(dst[:, halves[h]], banks[h][:, 0:HT], ACT.Tanh,
                                       bias=bias).then_inc(said.sem, 1)
                elif s == 4:
                    for h in range(2):
                        cs = slice(NR * h, NR * (h + 1))
                        act.wait_ge(biased4.sem, biased4.after(g, 2))
                        act.activation(by_tile(buf_a_g)[:, cs], by_tile(buf_b_g)[:, cs],
                                       ACT.Tanh).then_inc(tanh4.sem, 1)
                elif s == 5:
                    act.wait_ge(conv_done.sem, conv_done.after(g, 1))
                    act.copy(hres[g][:].rearrange("p j d -> p (j d)"),
                             banks[0][0:TOK, 0:NJ * D]).then_inc(hres_ready.sem, 1)
                elif s == 6:
                    square("T", g)

            def stage_a(g, s):
                if s == 0:
                    act.wait_ge(xn1_turned.sem, xn1_turned.after(g, 1))
                    act.copy(xn1_t[:], a0[:, 0:TO]).then_inc(xn1t_ready.sem, 1)
                elif s == 1:
                    act.wait_ge(qv_done.sem, qv_done.after(g, 1))
                    act.copy(q_t[:], a0[:, 0:TO]).then_inc(qt_ready.sem, 1)
                    act.wait_ge(qv_done.sem, qv_done.after(g, 2))
                    act.copy(v_s[:].rearrange("p r n -> p (r n)"), a1[0:TOK, 0:NR * P]).then_inc(v_ready.sem, 1)
                elif s in (2, 3):
                    b = s - 2
                    act.wait_ge(logit_done.sem, logit_done.after(g, b + 1))
                    act.activation(attn[:, b, TOK:TO], a0[0:TOK, TOK:TO], ACT.Relu).then_inc(off_ready.sem, 1)
                    act.wait_ge(diag_ready.sem, diag_ready.after(g, NR * b + 1))
                    act.activation(attn[:, b, TO + TOK:TO + 2 * TOK], a1[0:TOK, TOK:2 * TOK],
                                   ACT.Relu).then_inc(off_ready.sem, 1)
                elif s == 5:
                    square("A", g)
                elif s == 8:
                    for b in range(PAIR):
                        act.wait_ge(split_turned.sem, split_turned.after(g, b + 1))
                        act.copy(xs[g % 2][:, b, 0:TO], (a0, a1)[b][:, 0:TO]).then_inc(xs_ready.sem, 1)
                elif s == 10:
                    act.wait_ge(diff_ready.sem, diff_ready.after(g, 1))
                    act.activation(top[:, 3, :], top[:, 2, :], ACT.Exp).then_inc(exp_ready.sem, 1)
                elif s == 12:
                    act.wait_ge(gates_turned.sem, gates_turned.after(g, 1))
                    if g:
                        act.wait_ge(gates_out.sem, gates_out.after(g - 1, NR))
                    act.copy(gates_t[:], a1[0:NJ * E, 0:TOK]).then_inc(gates_t_ready.sem, 1)

            def stage_f(g, s):
                if s == 0:
                    act.wait_ge(y_added.sem, y_added.after(g, E))
                    act.copy(y_t[:], y[g % 2][:, 0:TO]).then_inc(yt_ready.sem, 1)
                elif s == 2:
                    square("F", g)

            def expert(g, e):
                if g == 0 and e == 0:
                    act.wait_ge(turned_ready, 2)
                n = E * g + e
                for b in range(PAIR):
                    act.wait_ge(z_done.sem, z_done.after(g, PAIR * e + b + 1))
                    if n >= REL:
                        gated = (hid0_ready, hid1_ready)[b]
                        act.wait_ge(gated.sem, n - REL + 1)
                    act.activation(rel[:, n % REL, b], z[e % 2][b][:, 0:TO], ACT.Relu,
                                   bias=b1_col[:, e:e + 1]).then_inc(rel_ready.sem, 1)

            walk({"S": setup, "T": stage_t, "A": stage_a, "F": stage_f, "in": expert})

        @block.gpsimd
        def _(pool):
            made = [0]

            def chain(ins):
                made[0] += 1
                ins.then_inc(pool_chain, 1)
                pool.wait_ge(pool_chain, made[0])

            nc.gpsimd.memset(w_tok[:], 0.0).then_inc(zeroed, 1)
            chain(nc.gpsimd.memset(ident[:], 0.0))
            nc.gpsimd.affine_select(out=ident[:], in_=ident[:], compare_op=ALU.not_equal, fill=1.0, base=0,
                                    pattern=[[-1, P]], channel_multiplier=1).then_inc(const_pool, 1)
            nc.gpsimd.memset(filt_row[:], 0.0).then_inc(zeroed, 1)
            pool.wait_ge(zeroed, 2)
            pool.dma_start(filt_row[0:1, MID:MID + TAPS], filt.unsqueeze(0)).then_inc(ld_filt, 16)
            nc.gpsimd.memset(w_qk[:], 0.0).then_inc(zeroed, 1)
            nc.gpsimd.memset(w_vo[:], 0.0).then_inc(zeroed, 1)
            chain(nc.gpsimd.memset(causal_cap[:], BIG))
            nc.gpsimd.affine_select(out=causal_cap[:], in_=causal_cap[:], compare_op=ALU.is_ge, fill=0.0, base=0,
                                    pattern=[[1, TOK]], channel_multiplier=-1).then_inc(const_pool, 1)
            pool.wait_ge(ld_filt, 16)
            pool.dma_start(filt_pad[:], filt_row[:]).then_inc(ld_filt, 16)
            nc.gpsimd.iota(row_pos[:], pattern=[[TOK, NR]], base=0, channel_multiplier=1).then_inc(const_pool, 1)
            nc.gpsimd.iota(prio_i[:], pattern=[[-1, E]], base=E, channel_multiplier=0).then_inc(const_pool, 1)
            nc.gpsimd.memset(minus_half[:], -0.5).then_inc(const_pool, 1)
            for buf in xs:
                nc.gpsimd.memset(buf[:, :, TO:W].bitcast(F32), 0.0).then_inc(const_pool, 1)
            pool.wait_ge(const_pool, 1)
            nc.gpsimd.tensor_copy(rep6[:], ident[0:E, 0:E].unsqueeze(1).broadcast_to([E, NJ, E])).then_inc(const_pool, 1)
            chain(nc.gpsimd.memset(centring[:], 0.0))
            for b in range(PAIR):
                chain(nc.gpsimd.memset(centring[b * D:(b + 1) * D, b * D:(b + 1) * D], -1.0 / D))
            nc.gpsimd.tensor_tensor(centring[:], centring[:], ident[:], ALU.add).then_inc(centring_ready, 1)
            pool.wait_ge(ld_filt, 32)
            shifts = bass.AP(filt_pad, 0, [[1, TOK], [1, BANDW]])
            pool.dma_start(band[:, 0:BANDW], shifts).then_inc(ld_band, 16)
            pool.dma_start(b2_s[:], b2).then_inc(ld_b2, 16)
            pool.dma_start(gate_bb[:, 0, :], gate_b.partition_broadcast(TOK)).then_inc(ld_gate_b, 16)
            pool.dma_start(gamma_b[:, 0, :], gamma.partition_broadcast(TOK)).then_inc(ld_last, 16)
            pool.dma_start(beta_b[:, 0, :], beta.partition_broadcast(TOK)).then_inc(ld_last, 16)
            pool.wait_ge(const_pool, 5)

            def setup(_, s):
                if s == 7:
                    pool.wait_ge(w1_ready, 1)
                    nc.gpsimd.tensor_tensor(w1_lo[:], w1_raw[:], w1_hi[:].bitcast(F32),
                                            ALU.subtract).then_inc(w1_ready, 1)

            def inverse_root(k, g):
                pool.wait_ge(ln_var[k].sem, ln_var[k].after(g, 1))
                nc.gpsimd.tensor_tensor(stat[k][:, 2, :], stat[k][:, 1, :], minus_half[:],
                                        ALU.pow).then_inc(ln_rstd[k].sem, 1)

            def stage_t(g, s):
                if s == 7:
                    inverse_root("T", g)

            def stage_a(g, s):
                if s == 6:
                    inverse_root("A", g)

            def stage_f(g, s):
                if s == 0:
                    if g == 0:
                        pool.wait_ge(ld_last, 32)
                    pool.wait_ge(ln_cent["A"].sem, ln_cent["A"].after(g, 1))
                    if g:
                        pool.wait_ge(y_out_ready.sem, y_out_ready.after(g - 1, 1))
                    nc.gpsimd.tensor_tensor(h2_beta[:], h2[g % 3][:], beta_b[:].broadcast_to([TOK, NJ, D]),
                                            ALU.add).then_inc(h2_beta_ready.sem, 1)
                elif s == 3:
                    inverse_root("F", g)

            def gate(g, e):
                n = E * g + e
                pool.wait_ge(rel_ready.sem, rel_ready.after(g, PAIR * e + 2))
                if e in CHUNKS:
                    k = CHUNKS.index(e)
                    pool.wait_ge(gate_all_ready[k].sem, gate_all_ready[k].after(g, 1))
                if n >= HID:
                    pool.wait_ge(y_added.sem, n - HID + 1)
                nc.gpsimd.tensor_tensor(hid[:, n % HID, 1], rel[:, n % REL, 1], gate_all[:, e, 1],
                                        ALU.mult).then_inc(hid1_ready.sem, 1)

            walk({"S": setup, "T": stage_t, "A": stage_a, "F": stage_f, "gate": gate})

        @block.vector
        def _(dve):
            class Chain:

                def __init__(self, sig):
                    self.sig, self.k, self.g = sig, 0, None

                def at(self, g):
                    if g != self.g:
                        assert self.k in (0, self.sig.per), (self.sig.sem, self.k)
                        self.g, self.k = g, 0
                    return self

                def __call__(self, ins):
                    self.k += 1
                    ins.then_inc(self.sig.sem, 1)
                    dve.wait_ge(self.sig.sem, self.sig.after(self.g, self.k))

            chains = {"T": Chain(t_chain), "A": Chain(a_chain), "F": Chain(f_chain)}

            def wide(ap, n=D):
                return ap.unsqueeze(2).broadcast_to([TOK, NJ, n])

            def center(k, g, src):
                link, st = chains[k].at(g), stat[k]
                link(nc.vector.tensor_reduce(st[:, 0, :], src[:], AX.X, ALU.add))
                nc.vector.scalar_tensor_tensor(out=cent[k][:], in0=wide(st[:, 0, :]), scalar=1.0 / D, in1=src[:],
                                               op0=ALU.mult, op1=ALU.subtract, reverse1=True)\
                    .then_inc(ln_cent[k].sem, 1)

            def variance(k, g):
                link, st = chains[k].at(g), stat[k]
                dve.wait_ge(ln_sq[k].sem, ln_sq[k].after(g, 1))
                link(nc.vector.tensor_reduce(st[:, 0, :], csq[k][:], AX.X, ALU.add))
                nc.vector.tensor_scalar(st[:, 1, :], st[:, 0, :], 1.0 / D, EPS, ALU.mult,
                                        ALU.add).then_inc(ln_var[k].sem, 1)

            def normalise(k, g, dst):
                dve.wait_ge(ln_rstd[k].sem, ln_rstd[k].after(g, 1))
                nc.vector.tensor_tensor(dst[:], cent[k][:], wide(stat[k][:, 2, :]), ALU.mult).then_inc(ln_done[k].sem, 1)

            def setup(_, s):
                if s == 8:
                    dve.wait_ge(vec_turned, 2)
                    dve.wait_ge(ld_out, 32)
                    nc.vector.scalar_tensor_tensor(out=core_abs[:], in0=vec_cols[:, 4:5], scalar=-1.0, in1=vec_cols[:, 4:5],
                                                   op0=ALU.mult, op1=ALU.max).then_inc(core_ready, 1)
                    dve.wait_ge(core_ready, 1)
                    nc.vector.tensor_scalar(w_tok[:, 3, :], w_tok[:, 3, :], core_abs[:, 0:1], None,
                                            ALU.mult).then_inc(core_ready, 1)
                elif s == 1:
                    dve.wait_ge(turned, 1)
                    nc.vector.tensor_copy(wo_t[:], a0[0:D, 0:D]).then_inc(turned_ready, 1)
                    nc.vector.tensor_copy(b1_col[:], a0[:, 128:128 + E]).then_inc(turned_ready, 1)
                elif s == 2:
                    dve.wait_ge(zeroed, 4)
                    dve.wait_ge(prod_done, 1)
                    for b in range(PAIR):
                        r = slice(b * D, (b + 1) * D)
                        nc.vector.tensor_copy(w_qk[r, r], a1[r, 0:D]).then_inc(prod_ready, 1)
                        nc.vector.tensor_copy(w_vo[r, r], a1[r, 128:128 + D]).then_inc(prod_ready, 1)
                elif s == 3:
                    dve.wait_ge(const_pool, 1)
                    nc.vector.tensor_reduce(own_tile[:], ident[0:NJ * E, 0:NJ * E].rearrange("p (j e) -> p j e", j=NJ),
                                            AX.X, ALU.add).then_inc(b2_diag_ready, 1)
                elif s == 4:
                    dve.wait_ge(b2_diag_ready, 1)
                    dve.wait_ge(b2_rows, 1)
                    rows = a0[0:NJ * E, 256:256 + D]
                    nc.vector.tensor_reduce(b2_mean[:], rows, AX.X, ALU.add).then_inc(b2_diag_ready, 1)
                    dve.wait_ge(b2_diag_ready, 2)
                    nc.vector.scalar_tensor_tensor(out=b2_cent[:], in0=b2_mean[:].broadcast_to([NJ * E, D]),
                                                   scalar=1.0 / D, in1=rows, op0=ALU.mult, op1=ALU.subtract,
                                                   reverse1=True).then_inc(b2_diag_ready, 1)
                    dve.wait_ge(b2_diag_ready, 3)
                    nc.vector.tensor_tensor(b2_diag[:], b2_cent[:].unsqueeze(1).broadcast_to([NJ * E, NJ, D]),
                                            own_tile[:].unsqueeze(2).broadcast_to([NJ * E, NJ, D]),
                                            ALU.mult).then_inc(b2_diag_ready, 1)
                elif s == 5:
                    dve.wait_ge(ld_band, 16)
                    for k in range(4):
                        nc.vector.tensor_copy(conv_w[:, k, :], conv_block(k)).then_inc(conv_w_ready, 1)
                elif s == 6:
                    dve.wait_ge(const_pool, 4)
                    nc.vector.tensor_scalar(row_cnt[:], row_pos[:], 1.0, None, ALU.max).then_inc(small, 1)
                    nc.vector.tensor_copy(prio[:, 0, :], prio_i[:]).then_inc(small, 1)
                    dve.wait_ge(ld_gate_b, 16)
                    dve.wait_ge(ld_gate, 32)
                    nc.vector.tensor_copy(gate_s[:, 0, :], gate_raw[:]).then_inc(small, 1)
                    dve.wait_ge(small, 3)
                    nc.vector.reciprocal(row_inv[:], row_cnt[:]).then_inc(small, 1)
                    nc.vector.tensor_tensor(gate_s[:, 1, :], gate_raw[:], gate_s[:, 0, :].bitcast(F32),
                                            ALU.subtract).then_inc(small, 1)
                    dve.wait_ge(small, 5)

            def stage_t(g, s):
                if s == 0:
                    for h in range(2):
                        dve.wait_ge(x_turned.sem, x_turned.after(g, h + 1))
                        nc.vector.tensor_copy(buf_a[g][:, halves[h]], banks_of(g)[h][:, 0:HT]).then_inc(xt_ready.sem, 1)
                elif s == 2:
                    for h in range(2):
                        dve.wait_ge(tanh2.sem, tanh2.after(g, h + 1))
                        nc.vector.tensor_tensor(buf_b[g][:, halves[h]], buf_a[g][:, halves[h]], buf_a[g][:, halves[h]],
                                                ALU.mult).then_inc(squared.sem, 1)
                elif s == 4:
                    if g == 0:
                        dve.wait_ge(ld_bias, 16)
                    flat = bias_last[:].rearrange("p b d -> p (b d)").unsqueeze(1).broadcast_to([TOK, NR, P])
                    for h in range(2):
                        dve.wait_ge(mm4.sem, mm4.after(g, h + 1))
                        sums = banks_of(g)[h][0:TOK, 0:NR * P].rearrange("p (c n) -> p c n", c=NR)
                        nc.vector.tensor_tensor(by_tile(buf_b[g])[:, NR * h:NR * (h + 1), :], sums, flat,
                                                ALU.add).then_inc(biased4.sem, 1)
                elif s == 6:
                    dve.wait_ge(hres_ready.sem, hres_ready.after(g, 1))
                    center("T", g, hres[g])
                elif s == 7:
                    variance("T", g)
                elif s == 8:
                    normalise("T", g, xn1[g])

            def pick_a(link, values, best):
                link(nc.vector.tensor_reduce(best, values, AX.X, ALU.max))
                link(nc.vector.tensor_tensor(work[:, 0], values, wide(best, E), ALU.is_equal))

            def pick_b(link, chosen):
                link(nc.vector.tensor_tensor(work[:, 1], work[:, 0], prio[:].broadcast_to([TOK, NJ, E]), ALU.mult))
                link(nc.vector.tensor_reduce(top[:, 4, :], work[:, 1], AX.X, ALU.max))
                link(nc.vector.tensor_tensor(chosen, work[:, 1], wide(top[:, 4, :], E), ALU.is_equal))

            def stage_a(g, s):
                link = chains["A"].at(g)
                first, second = top[:, 0, :], top[:, 1, :]
                if s in (2, 3):
                    b = s - 2
                    dve.wait_ge(logit_done.sem, logit_done.after(g, b + 1))
                    for o, src in ((TO, a1[0:TOK, 0:TOK]), (0, a0[0:TOK, 0:TOK]),
                                   (TO + 2 * TOK, a0[0:TOK, TO:TO + TOK])):
                        if o == 0:
                            dve.wait_ge(off_ready.sem, off_ready.after(g, 2 * b + 1))
                        nc.vector.scalar_tensor_tensor(out=attn[:, b, o:o + TOK], in0=src, scalar=0.0,
                                                       in1=causal_cap[:], op0=ALU.max,
                                                       op1=ALU.min).then_inc(diag_ready.sem, 1)
                elif s == 4:
                    dve.wait_ge(ctx_done.sem, ctx_done.after(g, 1))
                    for r in range(NR):
                        js = slice(PAIR * r, PAIR * (r + 1))
                        ins = nc.vector.scalar_tensor_tensor(
                            out=h2[g % 3][:, js, :].rearrange("p j d -> p (j d)"), in0=a0[0:TOK, r * P:(r + 1) * P],
                            scalar=row_inv[:, r:r + 1], in1=hres[g][:, js, :].rearrange("p j d -> p (j d)"),
                            op0=ALU.mult, op1=ALU.add)
                    link(ins)
                elif s == 5:
                    center("A", g, h2[g % 3])
                elif s == 6:
                    variance("A", g)
                elif s == 7:
                    normalise("A", g, xn2)
                    dve.wait_ge(ln_done["A"].sem, ln_done["A"].after(g, 1))
                    link(nc.vector.tensor_copy(split[:, :, 0, :], xn2[:]))
                    nc.vector.tensor_tensor(split[:, :, 1, :], xn2[:], split[:, :, 0, :].bitcast(F32),
                                            ALU.subtract).then_inc(split_ready.sem, 1)
                elif s == 9:
                    dve.wait_ge(gate_done.sem, gate_done.after(g, 1))
                    sums = a0[0:TOK, 0:NJ * 2 * E].rearrange("p (j s e) -> p j s e", s=2, e=E)
                    link(nc.vector.tensor_tensor(work[:, 3], sums[:, :, 1, :], gate_bb[:].broadcast_to([TOK, NJ, E]), ALU.add))
                    link(nc.vector.tensor_tensor(logits[:], sums[:, :, 0, :], work[:, 3], ALU.add))
                    pick_a(link, logits[:], first)
                    pick_b(link, pick1[:])
                elif s == 10:
                    link(nc.vector.scalar_tensor_tensor(out=work[:, 2], in0=pick1[:], scalar=-BIG, in1=logits[:],
                                                        op0=ALU.mult, op1=ALU.add))
                    pick_a(link, work[:, 2], second)
                    nc.vector.tensor_tensor(top[:, 2, :], second, first, ALU.subtract).then_inc(diff_ready.sem, 1)
                    pick_b(link, pick2[:])
                elif s == 11:
                    dve.wait_ge(exp_ready.sem, exp_ready.after(g, 1))
                    link(nc.vector.tensor_scalar(top[:, 5, :], top[:, 3, :], 1.0, None, ALU.add))
                    link(nc.vector.reciprocal(top[:, 6, :], top[:, 5, :]))
                    link(nc.vector.tensor_tensor(top[:, 7, :], top[:, 3, :], top[:, 6, :], ALU.mult))
                    link(nc.vector.tensor_tensor(work[:, 0], pick1[:], wide(top[:, 6, :], E), ALU.mult))
                    link(nc.vector.tensor_tensor(work[:, 1], pick2[:], wide(top[:, 7, :], E), ALU.mult))
                    nc.vector.tensor_tensor(gates[:], work[:, 0], work[:, 1], ALU.add).then_inc(gates_made.sem, 1)
                elif s == 13:
                    dve.wait_ge(b2_done.sem, b2_done.after(g, 1))
                    nc.vector.tensor_tensor(y_base[g % 2][:].rearrange("p j d -> p (j d)"), a0[0:TOK, 0:NJ * D],
                                            xn2[:].rearrange("p j d -> p (j d)"), ALU.add).then_inc(y_base_ready.sem, 1)

            def stage_f(g, s):
                link = chains["F"].at(g)
                if s == 2:
                    dve.wait_ge(y_turned.sem, y_turned.after(g, 1))
                    nc.vector.tensor_tensor(cent["F"][:].rearrange("p j d -> p (j d)"), y[g % 2][0:TOK, 0:NJ * D],
                                            y_base[g % 2][:].rearrange("p j d -> p (j d)"),
                                            ALU.add).then_inc(ln_cent["F"].sem, 1)
                elif s == 3:
                    variance("F", g)
                elif s == 4:
                    if g == 0:
                        dve.wait_ge(ld_last, 32)
                    dve.wait_ge(ln_cent["F"].sem, ln_cent["F"].after(g, 1))
                    link(nc.vector.tensor_tensor(scaled[:], cent["F"][:], gamma_b[:].broadcast_to([TOK, NJ, D]), ALU.mult))
                    dve.wait_ge(ln_rstd["F"].sem, ln_rstd["F"].after(g, 1))
                    link(nc.vector.tensor_tensor(yn[:], scaled[:], wide(stat["F"][:, 2, :]), ALU.mult))
                    dve.wait_ge(h2_beta_ready.sem, h2_beta_ready.after(g, 1))
                    if g:
                        dve.wait_ge(stored.sem, stored.after(g - 1, PAIR))
                    nc.vector.tensor_tensor(y_out[:], yn[:], h2_beta[:], ALU.add).then_inc(y_out_ready.sem, 1)

            def gate(g, e):
                n = E * g + e
                dve.wait_ge(rel_ready.sem, rel_ready.after(g, PAIR * e + 1))
                if e in CHUNKS:
                    k = CHUNKS.index(e)
                    dve.wait_ge(gate_all_ready[k].sem, gate_all_ready[k].after(g, 1))
                if n >= HID:
                    dve.wait_ge(y_added.sem, n - HID + 1)
                nc.vector.tensor_tensor(hid[:, n % HID, 0], rel[:, n % REL, 0], gate_all[:, e, 0],
                                        ALU.mult).then_inc(hid0_ready.sem, 1)

            walk({"S": setup, "T": stage_t, "A": stage_a, "F": stage_f, "gate": gate})

        @block.tensor
        def _(pe):
            mm = nc.tensor.matmul

            pe.wait_ge(const_pool, 1)

            def setup(_, s):
                if s == 8:
                    pe.wait_ge(ld_vec, 48)
                    nc.tensor.transpose(a1[:, 0:5], vec_rows[:].rearrange("n b d -> n (b d)"), ident[0:5, 0:5])\
                        .then_inc(vec_turned, 1)
                elif s == 1:
                    pe.wait_ge(ld_turn, 32)
                    nc.tensor.transpose(a0[0:D, 0:D], wo_s[:], ident[0:D, 0:D])
                    nc.tensor.transpose(a0[:, 128:128 + E], b1_s[:], ident[0:E, 0:E]).then_inc(turned, 1)
                elif s == 2:
                    pe.wait_ge(turned_ready, 2)
                    pe.wait_ge(vec_turned, 2)
                    pe.wait_ge(ld_attn, 48)
                    mm(a1[:, 0:D], wq2[:].rearrange("p b d -> p (b d)"), wk_s[:], start=True, stop=True)
                    mm(a1[:, 128:128 + D], wv2[:].rearrange("p b d -> p (b d)"), wo_t[:],
                       start=True, stop=True).then_inc(prod_done, 1)
                elif s == 4:
                    pe.wait_ge(ld_b2, 16)
                    pe.wait_ge(const_pool, 8)
                    mm(a0[0:NJ * E, 256:256 + D], rep6[:].rearrange("p j e -> p (j e)"), b2_s[:],
                       start=True, stop=True).then_inc(b2_rows, 1)

            def stage_t(g, s):
                banks = banks_of(g)
                if s == 0:
                    pe.wait_ge(x_in_ready[g], 16 * PAIR)
                    if g == 3:
                        pe.wait_ge(hres_ready.sem, hres_ready.after(0, 1))
                    for c in range(NT):
                        ins = nc.tensor.transpose(banks[c // NR][:, c % NR * TOK:(c % NR + 1) * TOK],
                                                  x_in[g % 2][:, c].rearrange("p b d -> p (b d)"), ident[0:TOK, 0:TOK])
                        if c % NR == NR - 1:
                            ins.then_inc(x_turned.sem, 1)
                elif s in (1, 2, 3):
                    if g == 0 and s == 1:
                        pe.wait_ge(ld_in, 32)
                    if g == 0 and s == 3:
                        pe.wait_ge(core_ready, 2)
                    src, ready, said = {1: (buf_a, xt_ready, mm1), 2: (buf_b, tanh1, mm2), 3: (buf_b, squared, mm3)}[s]
                    for h in range(2):
                        pe.wait_ge(ready.sem, ready.after(g, h + 1))
                        mm(banks[h][:, 0:HT], w_tok[:, (0, 1, 3)[s - 1], :], src[g][:, halves[h]],
                           start=True, stop=True).then_inc(said.sem, 1)
                elif s == 4:
                    for c in range(NT):
                        if c % NR == 0:
                            pe.wait_ge(tanh3.sem, tanh3.after(g, c // NR + 1))
                        ins = mm(banks[c // NR][0:TOK, c % NR * P:(c % NR + 1) * P],
                                 buf_a[g][:, c * TOK:(c + 1) * TOK], w_tok[:, 2, :], start=True, stop=True)
                        if c % NR == NR - 1:
                            ins.then_inc(mm4.sem, 1)
                elif s == 5:
                    if g == 0:
                        pe.wait_ge(conv_w_ready, 4)
                    pe.wait_ge(tanh4.sem, tanh4.after(g, 2))
                    for r in range(NR):
                        cs = [c for c in range(2 * r - 1, 2 * r + 3) if 0 <= c < NT]
                        for c in cs:
                            ins = mm(banks[0][0:TOK, r * P:(r + 1) * P], conv_w[:, c - 2 * r + 1, :],
                                     by_tile(buf_a[g])[:, c, :], start=c == cs[0], stop=c == cs[-1])
                    ins.then_inc(conv_done.sem, 1)

            def stage_a(g, s):
                if s == 0:
                    pe.wait_ge(ln_done["T"].sem, ln_done["T"].after(g, 1))
                    if g:
                        pe.wait_ge(y_base_ready.sem, y_base_ready.after(g - 1, 1))
                    else:
                        pe.wait_ge(b2_diag_ready, 4)
                    for r in range(NR):
                        ins = nc.tensor.transpose(a0[:, r * TOK:(r + 1) * TOK],
                                                  xn1[g][:, PAIR * r:PAIR * (r + 1)].rearrange("p b d -> p (b d)"),
                                                  ident[0:TOK, 0:TOK])
                    ins.then_inc(xn1_turned.sem, 1)
                elif s == 1:
                    if g == 0:
                        pe.wait_ge(prod_ready, 2 * PAIR)
                    pe.wait_ge(xn1t_ready.sem, xn1t_ready.after(g, 1))
                    mm(a0[:, 0:TO], w_qk[:], xn1_t[:], start=True, stop=True).then_inc(qv_done.sem, 1)
                    if g:
                        pe.wait_ge(gates_t_ready.sem, gates_t_ready.after(g - 1, 1))
                    for r in range(NR):
                        ins = mm(a1[0:TOK, r * P:(r + 1) * P], xn1_t[:, r * TOK:(r + 1) * TOK], w_vo[:],
                                 start=True, stop=True)
                    ins.then_inc(qv_done.sem, 1)
                elif s in (2, 3):
                    b = s - 2
                    if b == 0:
                        pe.wait_ge(qt_ready.sem, qt_ready.after(g, 1))
                        pe.wait_ge(v_ready.sem, v_ready.after(g, 1))
                    else:
                        pe.wait_ge(off_ready.sem, off_ready.after(g, 2))
                        pe.wait_ge(diag_ready.sem, diag_ready.after(g, NR))
                    f = slice(b * D, (b + 1) * D)
                    for m, dst in ((0, a0[0:TOK, 0:TO]), (1, a1[0:TOK, 0:2 * TOK]), (2, a0[0:TOK, TO:TO + TOK])):
                        ins = mm(dst, xn1_t[f, m * TOK:(m + 1) * TOK], q_t[f, m * TOK:TO], start=True, stop=True)
                    ins.then_inc(logit_done.sem, 1)
                elif s == 4:
                    pe.wait_ge(off_ready.sem, off_ready.after(g, 2 * PAIR))
                    pe.wait_ge(diag_ready.sem, diag_ready.after(g, NR * PAIR))
                    at = [0, TO, TO + 2 * TOK]
                    for r in range(NR):
                        for b in range(PAIR):
                            for m in range(r + 1):
                                ins = mm(a0[0:TOK, r * P + b * D:r * P + (b + 1) * D],
                                         attn[:, b, at[m] + (r - m) * TOK:at[m] + (r - m + 1) * TOK],
                                         v_s[:, m, b * D:(b + 1) * D], start=m == 0, stop=m == r)
                    ins.then_inc(ctx_done.sem, 1)
                elif s == 8:
                    pe.wait_ge(split_ready.sem, split_ready.after(g, 1))
                    for b in range(PAIR):
                        for r in range(NR):
                            ins = nc.tensor.transpose(
                                (a0, a1)[b][:, r * TOK:(r + 1) * TOK],
                                split[:, PAIR * r + b].rearrange("p s d -> p (s d)").bitcast(F32),
                                ident[0:TOK, 0:TOK])
                        ins.then_inc(split_turned.sem, 1)
                elif s == 9:
                    if g == 0:
                        pe.wait_ge(small, 5)
                    pe.wait_ge(xs_ready.sem, xs_ready.after(g, PAIR))
                    for j in range(NJ):
                        r, b = j // PAIR, j % PAIR
                        ins = mm(a0[0:TOK, j * 2 * E:(j + 1) * 2 * E], xs[g % 2][:, b, r * TOK:(r + 1) * TOK],
                                 gate_s[:].rearrange("p s e -> p (s e)"), start=True, stop=True)
                    ins.then_inc(gate_done.sem, 1)
                elif s == 12:
                    pe.wait_ge(gates_made.sem, gates_made.after(g, 1))
                    nc.tensor.transpose(a1[0:NJ * E, 0:TOK], gates[:].rearrange("p j e -> p (j e)"),
                                        ident[0:TOK, 0:TOK]).then_inc(gates_turned.sem, 1)
                elif s == 13:
                    pe.wait_ge(gates_t_ready.sem, gates_t_ready.after(g, 1))
                    mm(a0[0:TOK, 0:NJ * D], gates_t[:], b2_diag[:].rearrange("p j d -> p (j d)"),
                       start=True, stop=True).then_inc(b2_done.sem, 1)

            def stage_f(g, s):
                if s == 1:
                    if g == 0:
                        pe.wait_ge(centring_ready, 1)
                    pe.wait_ge(yt_ready.sem, yt_ready.after(g, 1))
                    for r in range(NR):
                        ins = mm(y[g % 2][0:TOK, r * P:(r + 1) * P], y_t[:, r * TOK:(r + 1) * TOK], centring[:],
                                 start=True, stop=True)
                    ins.then_inc(y_turned.sem, 1)

            def expert_in(g, e):
                if e == 0:
                    pe.wait_ge(xs_ready.sem, xs_ready.after(g, PAIR))
                    if g == 0:
                        pe.wait_ge(w1_ready, 2)
                        pe.wait_ge(hres_ready.sem, hres_ready.after(1, 1))
                if g == 0 and e == 1:
                    pe.wait_ge(hres_ready.sem, hres_ready.after(NG - 1, 1))
                for b in range(PAIR):
                    if g or e >= 2:
                        pe.wait_ge(rel_ready.sem, rel_ready.after(g, PAIR * (e - 2) + b + 1))
                    mm(z[e % 2][b][:, 0:W], w1_hi[:, e, :], xs[g % 2][:, b, :], start=True, stop=False)
                    mm(z[e % 2][b][:, 0:W], w1_lo[:, e, :], xs[g % 2][:, b, :], start=False, stop=True).then_inc(z_done.sem, 1)

            def expert_out(g, e):
                pe.wait_ge(hid0_ready.sem, hid0_ready.after(g, e + 1))
                pe.wait_ge(hid1_ready.sem, hid1_ready.after(g, e + 1))
                if g == 0 and e == 0:
                    pe.wait_ge(ld_w2, 16)
                if g >= 2 and e == 0:
                    pe.wait_ge(ln_cent["F"].sem, ln_cent["F"].after(g - 2, 1))
                for b in range(PAIR):
                    ins = mm(y[g % 2][b * D:(b + 1) * D, 0:TO], w2_s[:, e, :], hid[:, (E * g + e) % HID, b],
                             start=e == 0, stop=e == E - 1)
                ins.then_inc(y_added.sem, 1)

            walk({"S": setup, "T": stage_t, "A": stage_a, "F": stage_f, "in": expert_in, "out": expert_out})


_INS = ["x", "L0_tok_W_in", "L0_tok_b_in", "L0_tok_W_out", "L0_tok_b_out", "L0_tok_core_diag", "L0_tok_conv_filter",
        "L0_attn_Wq", "L0_attn_Wk", "L0_attn_Wv", "L0_attn_Wo", "L0_ffn_gate_w", "L0_ffn_gate_b", "L0_ffn_w1",
        "L0_ffn_b1", "L0_ffn_w2", "L0_ffn_b2", "L0_ffn_gamma", "L0_ffn_beta"]
_OUT = ((8, 375, 64), "float32")


def kernel(**inputs):
    import numpy as _np
    import concourse.bacc as _bacc
    from concourse import mybir as _mybir
    from concourse.bass_utils import run_bass_kernel_spmd as _run

    nc = _bacc.Bacc("TRN2", target_bir_lowering=False, num_devices=1)
    arrays, args = {}, []
    for name in _INS:
        a = _np.ascontiguousarray(inputs[name])
        arrays[f"in_{name}_dram"] = a
        args.append(nc.dram_tensor(f"in_{name}_dram", a.shape, _mybir.dt.from_np(a.dtype), kind="ExternalInput").ap())
    args.append(nc.dram_tensor("out_dram", _OUT[0], _mybir.dt.from_np(_np.dtype(_OUT[1])), kind="ExternalOutput").ap())
    audio_tower(nc, *args)
    r = _run(nc, [arrays], core_ids=[0])
    return r.results[0]["out_dram"]
```
